# Optimizing a Trainium2 kernel written in Bass

```python
import numpy as np
import jax
import jax.numpy as jnp

def _softmax(x, axis=-1):
    return jax.nn.softmax(x, axis=axis)

def _gelu(x):
    return jax.nn.gelu(x, approximate=True)

def _silu(x):
    return jax.nn.silu(x)

def _sigmoid(x):
    return jax.nn.sigmoid(x)

def _layernorm(x, axis=-1, eps=1e-05):
    m = jnp.mean(x, axis=axis, keepdims=True)
    v = jnp.var(x, axis=axis, keepdims=True)
    return (x - m) / jnp.sqrt(v + eps)

def _scatter_add(tgt, idx, src, axis=0):
    return tgt.at[idx].add(src)

def _segment_sum(src, seg, n):
    return jax.ops.segment_sum(src, seg, n)
kernel_name = 'mk_gnn_preln_d2_gnn_r32_9a7814'

def setup_inputs(seed: int=0):
    np.random.seed(seed)
    _w = jnp.asarray

    def _rec_inputs():
        import jax
        import jax.numpy as jnp
        _gk = jax.random.key(seed)
        x = -0.000202 + 1 * jax.random.normal(jax.random.fold_in(_gk, 1), (50000, 128), jnp.float32)
        src = jax.random.randint(jax.random.fold_in(_gk, 2), (25000,), 0, 50000, jnp.int32)
        dst = jax.random.randint(jax.random.fold_in(_gk, 3), (25000,), 0, 50000, jnp.int32)
        _o = jnp.argsort(dst, stable=True)
        src = src[_o]
        dst = dst[_o]
        edge_attr_128 = -5.16925e-05 + 1.00005 * jax.random.normal(jax.random.fold_in(_gk, 13), (25000, 128), jnp.float32)
        return (x, src, dst, edge_attr_128)
    x, src, dst, edge_attr_128 = _rec_inputs()

    def _L0_gnn_setup():
        import jax, jax.numpy as jnp
        import numpy as np
        N_NODES = 50000
        N_EDGES = 25000
        D = 128
        key = jax.random.key(seed)
        k1, k2, k3, k4 = jax.random.split(key, 4)
        feat = jax.random.normal(k1, (N_NODES, D), dtype=jnp.float32)
        W = jax.random.normal(k2, (D, D), dtype=jnp.float32) * (1.0 / np.sqrt(D))
        b = jnp.zeros((D,), dtype=jnp.float32)
        eps = jnp.zeros((1,), dtype=jnp.float32)
        src = jax.random.randint(k3, (N_EDGES,), 0, N_NODES, dtype=jnp.int64 if jax.config.jax_enable_x64 else jnp.int32)
        dst = jax.random.randint(k4, (N_EDGES,), 0, N_NODES, dtype=jnp.int64 if jax.config.jax_enable_x64 else jnp.int32)
        return {'feat': feat, 'W': W, 'b': b, 'eps': eps, 'src': src, 'dst': dst}
    _L0_gnn_all = _L0_gnn_setup()
    _L0_gnn_in = {k: v for k, v in _L0_gnn_all.items() if k in ('W', 'b', 'eps')}
    del _L0_gnn_all

    def _L1_gnn_setup():
        import jax, jax.numpy as jnp
        import numpy as np
        N, E, B = (50000, 25000, 16)
        DX = DE = DU = DO = 128
        IN1 = 2 * DX + DE + DU
        IN2 = DX + DO + DU
        key = jax.random.key(seed)
        ks = jax.random.split(key, 9)
        x = jax.random.normal(ks[0], (N, DX), dtype=jnp.float32)
        edge_index = jax.random.randint(ks[1], (2, E), 0, N, dtype=jnp.int64)
        edge_attr = jax.random.normal(ks[2], (E, DE), dtype=jnp.float32)
        u = jax.random.normal(ks[3], (B, DU), dtype=jnp.float32)
        batch = jnp.sort(jax.random.randint(ks[4], (N,), 0, B, dtype=jnp.int64))
        W1 = jax.random.normal(ks[5], (DO, IN1), dtype=jnp.float32) / np.sqrt(IN1)
        b1 = jnp.zeros((DO,), dtype=jnp.float32)
        W2 = jax.random.normal(ks[6], (DO, IN2), dtype=jnp.float32) / np.sqrt(IN2)
        b2 = jnp.zeros((DO,), dtype=jnp.float32)
        return {'x': x, 'edge_index': edge_index, 'edge_attr': edge_attr, 'u': u, 'batch': batch, 'W1': W1, 'b1': b1, 'W2': W2, 'b2': b2}
    _L1_gnn_all = _L1_gnn_setup()
    _L1_gnn_in = {k: v for k, v in _L1_gnn_all.items() if k in ('u', 'W1', 'b1', 'W2', 'b2')}
    del _L1_gnn_all
    return {'x': x, 'src': src, 'dst': dst, 'edge_attr_128': edge_attr_128, 'L0_gnn_W': _L0_gnn_in['W'], 'L0_gnn_b': _L0_gnn_in['b'], 'L0_gnn_eps': _L0_gnn_in['eps'], 'L1_gnn_u': _L1_gnn_in['u'], 'L1_gnn_W1': _L1_gnn_in['W1'], 'L1_gnn_b1': _L1_gnn_in['b1'], 'L1_gnn_W2': _L1_gnn_in['W2'], 'L1_gnn_b2': _L1_gnn_in['b2']}

def reference(x, src, dst, edge_attr_128, L0_gnn_W, L0_gnn_b, L0_gnn_eps, L1_gnn_u, L1_gnn_W1, L1_gnn_b1, L1_gnn_W2, L1_gnn_b2):
    import jax
    import jax.numpy as jnp

    def _L0_gnn_ref(feat, W, b, eps, src, dst):
        import jax, jax.numpy as jnp
        import numpy as np
        N_NODES = 50000
        N_EDGES = 25000
        D = 128
        msgs = feat[src]
        neigh = jax.ops.segment_sum(msgs, dst, num_segments=N_NODES)
        rst = (1.0 + eps) * feat + neigh
        out = jnp.einsum('nd,de->ne', rst, W) + b
        return out

    def _L1_gnn_ref(x, edge_index, edge_attr, u, batch, W1, b1, W2, b2):
        import jax, jax.numpy as jnp
        import numpy as np
        N, E, B = (50000, 25000, 16)
        DX = DE = DU = DO = 128
        IN1 = 2 * DX + DE + DU
        IN2 = DX + DO + DU
        col, row = (edge_index[0], edge_index[1])
        msg_in = jnp.concatenate([x[row], x[col], edge_attr, u[batch[row]]], axis=1)
        edge_messages = jax.nn.relu(msg_in @ W1.T + b1)
        aggregated = jax.ops.segment_sum(edge_messages, row, num_segments=x.shape[0])
        node_in = jnp.concatenate([x, aggregated, u[batch]], axis=1)
        return jax.nn.relu(node_in @ W2.T + b2)
    edge_index = jnp.stack([src, dst])
    batch0 = jnp.zeros((50000,), jnp.int32)
    h = jnp.maximum(_layernorm(x, axis=-1), 0.0)
    x = x + _L0_gnn_ref(h, L0_gnn_W, L0_gnn_b, L0_gnn_eps, src, dst)
    h = jnp.maximum(_layernorm(x, axis=-1), 0.0)
    x = x + _L1_gnn_ref(h, edge_index, edge_attr_128, L1_gnn_u, batch0, L1_gnn_W1, L1_gnn_b1, L1_gnn_W2, L1_gnn_b2)
    return x

_drawn_inputs = setup_inputs


def setup_inputs(seed=0):
    import zlib

    import numpy as np

    out = dict(_drawn_inputs(seed))
    spreads = {'L0_gnn_b': (0.0, 0.1), 'L1_gnn_b1': (0.0, 0.592), 'L1_gnn_b2': (0.0, 0.1)}
    factors = {}
    for name, (base, spread) in spreads.items():
        noise = np.random.default_rng([zlib.crc32(name.encode()), seed]).standard_normal(out[name].shape)
        drawn = base * np.exp(spread * noise) if base else spread * noise
        out[name] = jnp.asarray(drawn.astype(out[name].dtype))
    for name, factor in factors.items():
        out[name] = (out[name] * factor).astype(out[name].dtype)
    return out
```

```python
from contextlib import ExitStack

import concourse.bass as bass
from concourse import mybir

ALU = mybir.AluOpType
ACT = mybir.ActivationFunctionType
AX = mybir.AxisListType
F32 = mybir.dt.float32
I32 = mybir.dt.int32

P = 128
ROWS = 4
BATCH = P * ROWS
PAIR = 2 * P
UNROLL = 4
BAND_BELOW = 2
BAND_ABOVE = 2
LN_EPS = 1e-5


class Plan:

    def __init__(self, count, dense0=None, edge0=None):
        self.count, self.dense0, self.edge0 = count, dense0, edge0
        ends = [b + count for b in (dense0, edge0) if b is not None]
        self.steps = max(ends)

    def has_dense(self, s):
        return self.dense0 is not None and self.dense0 <= s < self.dense0 + self.count

    def has_edge(self, s):
        return self.edge0 is not None and self.edge0 <= s < self.edge0 + self.count

    def pattern(self, tick, reach):
        near = []
        for s in range(tick - reach, tick + reach + 1):
            near.append((self.has_dense(s), self.has_edge(s),
                         self.dense0 is not None and s == self.dense0 + self.count - 1,
                         self.edge0 is not None and s == self.edge0 + self.count - 1))
        return near


class Step:

    def __init__(self, plan, turn, slot, known):
        self.plan, self.turn, self.slot, self.known = plan, turn, slot, known

    def at(self, offset):
        s = self.slot + offset
        return Step(self.plan, self.turn + s // UNROLL, s % UNROLL, self.known + offset)

    @property
    def number(self):
        return self.turn * UNROLL + self.slot

    @property
    def dense(self):
        return self.plan.has_dense(self.known)

    @property
    def edge(self):
        return self.plan.has_edge(self.known)

    @property
    def batch(self):
        return self.number - self.plan.dense0

    @property
    def pair(self):
        return self.number - self.plan.edge0

    @property
    def last_batch(self):
        return self.known == self.plan.dense0 + self.plan.count - 1

    @property
    def last_pair(self):
        return self.known == self.plan.edge0 + self.plan.count - 1


def count_before(step, start, per=1):
    return (step.number - start) * per


def uses_of_slot(step, start):
    first = start + (step.known - start) % UNROLL
    return (step.number - first) // UNROLL + 1 if isinstance(step.turn, int) else \
        step.turn + (step.slot - first) // UNROLL + 1


def run_steps(eng, plan, body, reach=4):
    tick, end = -reach, plan.steps + reach
    while tick < end:
        run = tick
        while run < end and plan.pattern(run, reach) == plan.pattern(tick, reach):
            run += 1
        start = tick + (-tick) % UNROLL
        turns = max(0, (run - start) // UNROLL)
        if turns >= 2 and tick >= 0:
            for s in range(tick, start):
                body(Step(plan, s // UNROLL, s % UNROLL, s))
            with eng.Fori(start // UNROLL, start // UNROLL + turns) as turn:
                for slot in range(UNROLL):
                    body(Step(plan, turn, slot, start + slot))
            tick = start + UNROLL * turns
        else:
            body(Step(plan, tick // UNROLL, tick % UNROLL, tick))
            tick += 1


def gnn_kernel(nc, x, src, dst, edge_attr, W0, b0, eps, u, W1, b1, W2, b2, out):
    N, D = x.shape
    E = src.shape[0]
    assert D == P
    n_batch = -(-N // BATCH)
    n_pair = -(-E // PAIR)
    assert n_batch == n_pair <= P
    tail_nodes = N - (n_batch - 1) * BATCH
    tail_rows = next(r for r in range(ROWS, 0, -1) if tail_nodes % (16 * r) == 0)
    tail_parts = tail_nodes // tail_rows
    assert tail_parts <= P
    tail_edges = E - (n_pair - 1) * PAIR
    assert P < tail_edges < PAIR
    pad_edges = n_pair * PAIR - E

    x1_dram = nc.dram_tensor("x1_scratch", (N + 2 * P, D), F32, kind="Internal").ap()
    agg_dram = nc.dram_tensor("agg_scratch", (N + 2 * P, D), F32, kind="Internal").ap()
    dst_dram = nc.dram_tensor("dst_padded", (n_pair * PAIR,), I32, kind="Internal").ap()
    src_dram = nc.dram_tensor("src_padded", (n_pair * PAIR,), I32, kind="Internal").ap()

    with ExitStack() as ctx:
        def sb(name, shape, dt=F32):
            return ctx.enter_context(nc.sbuf_tensor(name, shape, dt))

        def sem(name):
            return ctx.enter_context(nc.semaphore(name))

        ident = sb("ident", [P, P])
        later = sb("later", [P, PAIR])
        ones_row = sb("ones_row", [1, P])
        w0_node = sb("w0_node", [P, P])
        w0_edge = sb("w0_edge", [P, P])
        w1T = sb("w1T", [P, 4, P])
        w2T = sb("w2T", [P, 3, P])
        c1_row = sb("c1_row", [1, 2, P])
        c2_fill = sb("c2_fill", [P, ROWS, P])
        eps_ln = sb("eps_ln", [P, 1])
        dst_f = sb("dst_f", [P, n_pair, 2])
        to_dump = sb("to_dump", [P, n_pair, 2])
        index = sb("index", [P, n_pair, 6], I32)
        same = sb("same", [P, n_pair, 3 * P])
        fast = sb("fast", [1, 1], I32)

        X = sb("X", [P, UNROLL, 8, P])
        H = sb("H", [P, 2, 8, P])
        stats = sb("stats", [P, 2, 8, 6])
        total = sb("total", [P, 2, 8])
        gap = sb("gap", [P, 2, 8])
        spread = sb("spread", [P, 2, 8])
        sd = sb("sd", [P, 2, 8])
        rstd = sb("rstd", [P, 2, 8])
        nmr = sb("nmr", [P, 2, 8])
        hT = sb("hT", [P, ROWS, P])
        eT = sb("eT", [P, 6, P])
        sumT = sb("sumT", [P, 2, P])
        msg = sb("msg", [P, 2, P])
        edge_out = sb("edge_out", [P, 2, 2, P])
        node_out = sb("node_out", [P, 2, ROWS, P])
        agg_in = sb("agg_in", [P, 2, ROWS, P])
        attr = sb("attr", [P, UNROLL, 2, P])
        dst_row = attr[:, :, :, :].rearrange("p s h d -> p s (h d)").bitcast(I32)
        b0_row = agg_in[0:1, 0, :, :]
        masked = agg_in[:, 1, 0:2, :].rearrange("p a c -> p (a c)")
        n_later = sb("n_later", [P, 2, 2])
        moved = sb("moved", [P, 2])
        gather_at = sb("gather_at", [P, UNROLL, 4], I32)
        scatter_at = sb("scatter_at", [P, UNROLL, 2], I32)

        bank = [ctx.enter_context(nc.psum_tensor(f"bank{i}", [P, 4, P], F32)) for i in range(8)]

        w1_in, w2_in = hT, eT
        pair_i = [X[0:n_pair, 0, 0:2, :].bitcast(I32), X[0:n_pair, 0, 2:4, :].bitcast(I32)]
        pair_f = [X[0:n_pair, 1, 0:2, :], X[0:n_pair, 1, 2:4, :]]
        equal = eT[:, :, :].rearrange("p (q c) d -> p q (c d)", q=2)
        u_col = sb("u_col", [P, 1])
        u_wide = H[:, 0, 0, :]
        eps_col = sb("eps_col", [P, 1])
        brow = H[0:1, 1, 0:2, :]
        pad_dst = sb("pad_dst", [1, pad_edges], I32)
        pad_src = sb("pad_src", [1, pad_edges], I32)
        dump_i = sb("dump_i", [P, 2], I32)
        dump_f = sb("dump_f", [P, 2])
        base_i = sb("base_i", [P, 1], I32)
        base_f = sb("base_f", [P, 1])
        bound = sb("bound", [P, 4])
        ok = sb("ok", [P, 1])
        ones_col = sb("ones_col", [P, 1])
        zero_row = H[:, 0, 1, :]

        with ExitStack() as setup:
            def ssem(name):
                return setup.enter_context(nc.semaphore(name))

            weights_in = ssem("weights_in")
            rows_in = ssem("rows_in")
            pads_ready = ssem("pads_ready")
            padded = ssem("padded")
            pairs_in = ssem("pairs_in")
            dump_zeroed = ssem("dump_zeroed")
            consts = ssem("consts")
            dve_consts = ssem("dve_consts")
            pairs_f = ssem("pairs_f")
            turned = ssem("turned")
            w_ready = ssem("w_ready")
            biased = ssem("biased")
            chain = ssem("chain")
            counted = ssem("counted")
            block = setup.enter_context(nc.Block())

            @block.sync
            def _(sp):
                sp.dma_start(w1_in[:, :, :], W1.rearrange("o (c k) -> o c k", c=4)).then_inc(weights_in, 16)
                sp.dma_start(w2_in[:, 0:3, :], W2.rearrange("o (c k) -> o c k", c=3)).then_inc(weights_in, 16)
                sp.dma_start(w0_edge[:, :], W0).then_inc(weights_in, 16)
                with nc.allow_non_contiguous_dma(reason="one vector, a number to a partition"):
                    sp.dma_start(u_col[:, :], u[0:1, :].rearrange("a d -> d a")).then_inc(weights_in, 16)
                sp.dma_start(eps_col[:, :], eps.rearrange("(a d) -> a d", a=1).partition_broadcast(P)).then_inc(weights_in, 16)
                for r in range(ROWS):
                    sp.dma_start(b0_row[:, r, :], b0.rearrange("(a d) -> a d", a=1)).then_inc(rows_in, 16)
                sp.dma_start(brow[:, 0, :], b1.rearrange("(a d) -> a d", a=1)).then_inc(rows_in, 16)
                sp.dma_start(brow[:, 1, :], b2.rearrange("(a d) -> a d", a=1)).then_inc(rows_in, 16)
                sp.dma_start(dst_dram[0:E], dst).then_inc(padded, 16)
                sp.dma_start(src_dram[0:E], src).then_inc(padded, 16)
                sp.wait_ge(pads_ready, 2)
                sp.dma_start(dst_dram[E:n_pair * PAIR], pad_dst[0:1, :]).then_inc(padded, 16)
                sp.dma_start(src_dram[E:n_pair * PAIR], pad_src[0:1, :]).then_inc(padded, 16)
                sp.wait_ge(padded, 64)
                for t, of in enumerate((src_dram, dst_dram)):
                    sp.dma_start(pair_i[t], of.rearrange("(q h e) -> q h e", h=2, e=P)).then_inc(pairs_in, 16)
                sp.wait_ge(dve_consts, 4)
                for h in range(2):
                    sp.dma_start(x1_dram[N + h * P:N + (h + 1) * P, :], zero_row).then_inc(dump_zeroed, 16)
                for h in range(2):
                    sp.dma_start(agg_dram[N + h * P:N + (h + 1) * P, :], zero_row).then_inc(dump_zeroed, 16)
                sp.wait_ge(dump_zeroed, 64)

            @block.gpsimd
            def _(pool):
                nc.gpsimd.iota(pad_dst[:, :], pattern=[[1, pad_edges]], base=N + 2 * P - pad_edges,
                               channel_multiplier=0).then_inc(pads_ready, 1)
                nc.gpsimd.memset(pad_src[:, :], 0).then_inc(pads_ready, 1)
                nc.gpsimd.iota(dump_i[:, :], pattern=[[P, 2]], base=N, channel_multiplier=1).then_inc(consts, 1)
                nc.gpsimd.iota(base_i[:, :], pattern=[[0, 1]], base=0, channel_multiplier=BATCH).then_inc(consts, 1)
                pool.wait_ge(dve_consts, 2)
                nc.gpsimd.affine_select(out=ident[:, :], in_=ident[:, :], compare_op=ALU.not_equal, fill=1.0,
                                        base=0, pattern=[[-1, P]], channel_multiplier=1).then_inc(consts, 1)
                nc.gpsimd.affine_select(out=later[:, :], in_=later[:, :], compare_op=ALU.is_gt, fill=0.0,
                                        base=0, pattern=[[1, PAIR]], channel_multiplier=-1).then_inc(consts, 1)

            @block.tensor
            def _(pe):
                pe.wait_ge(consts, 4)
                pe.wait_ge(weights_in, 80)
                for c in range(4):
                    nc.tensor.transpose(bank[0][:, c, :], w1_in[:, c, :], ident[:, :])
                for c in range(3):
                    last = nc.tensor.transpose(bank[1][:, c, :], w2_in[:, c, :], ident[:, :])
                last.then_inc(turned, 1)
                pe.wait_ge(pairs_f, 2)
                for t in range(2):
                    for h in range(2):
                        last = nc.tensor.transpose(bank[2][:, 2 * t + h, 0:n_pair], pair_f[t][:, h, :],
                                                   ident[0:n_pair, 0:n_pair])
                last.then_inc(turned, 1)
                pe.wait_ge(w_ready, 3)
                pe.wait_ge(rows_in, 16 * (ROWS + 2))
                pe.wait_ge(dve_consts, 5)
                for c, wu in enumerate((w1T[:, 3, :], w2T[:, 2, :])):
                    nc.tensor.matmul(bank[3][:, c, :], u_wide, wu, start=True, stop=False)
                    last = nc.tensor.matmul(bank[3][:, c, :], ones_row[:, :], brow[:, c, :], start=False, stop=True)
                last.then_inc(biased, 1)
                pe.wait_ge(chain, 6)
                nc.tensor.matmul(bank[4][0:1, 0, 0:1], ok[0:n_pair, :], ones_col[0:n_pair, :],
                                 start=True, stop=True).then_inc(counted, 1)

            @block.vector
            def _(dve):
                nc.vector.memset(ident[:, :], 0.0).then_inc(dve_consts, 1)
                nc.vector.memset(later[:, :], 1.0).then_inc(dve_consts, 1)
                nc.vector.memset(ones_col[:, :], 1.0).then_inc(dve_consts, 1)
                nc.vector.memset(zero_row, 0.0).then_inc(dve_consts, 1)
                nc.vector.memset(ones_row[:, :], 1.0).then_inc(dve_consts, 1)
                nc.vector.memset(eps_ln[:, :], LN_EPS).then_inc(dve_consts, 1)
                dve.wait_ge(pairs_in, 32)
                for t in range(2):
                    nc.vector.tensor_copy(pair_f[t], pair_i[t]).then_inc(pairs_f, 1)
                dve.wait_ge(consts, 4)
                nc.vector.tensor_copy(dump_f[:, :], dump_i[:, :]).then_inc(chain, 1)
                nc.vector.tensor_copy(base_f[:, :], base_i[:, :]).then_inc(chain, 1)
                dve.wait_ge(pairs_f, 2)
                nc.vector.tensor_reduce(bound[0:n_pair, 0:1], pair_f[1], AX.XY, ALU.max).then_inc(chain, 1)
                nc.vector.tensor_reduce(bound[0:n_pair, 1:2], pair_f[1], AX.XY, ALU.min).then_inc(chain, 1)
                dve.wait_ge(chain, 4)
                nc.vector.tensor_scalar(bound[0:n_pair, 2:3], bound[0:n_pair, 0:1], base_f[0:n_pair, :],
                                        float((BAND_ABOVE + 1) * BATCH), ALU.subtract, ALU.is_lt).then_inc(chain, 1)
                dve.wait_ge(chain, 5)
                nc.vector.tensor_scalar(bound[0:n_pair, 3:4], bound[0:n_pair, 1:2], base_f[0:n_pair, :],
                                        float(-BAND_BELOW * BATCH), ALU.subtract, ALU.is_ge).then_inc(w_ready, 1)
                dve.wait_ge(w_ready, 1)
                nc.vector.tensor_tensor(ok[0:n_pair, :], bound[0:n_pair, 2:3], bound[0:n_pair, 3:4],
                                        ALU.mult).then_inc(chain, 1)
                dve.wait_ge(weights_in, 80)
                nc.vector.tensor_scalar(u_wide, zero_row, u_col[:, :], None, ALU.add).then_inc(w_ready, 1)
                nc.vector.tensor_scalar(eps_col[:, :], eps_col[:, :], 1.0, None, ALU.add).then_inc(chain, 1)
                dve.wait_ge(turned, 1)
                nc.vector.tensor_copy(w1T[:, :, :], bank[0][:, :, :])
                nc.vector.tensor_copy(w2T[:, :, :], bank[1][:, 0:3, :]).then_inc(w_ready, 1)
                dve.wait_ge(chain, 7)
                nc.vector.tensor_scalar(w0_node[:, :], w0_edge[:, :], eps_col[:, :], None, ALU.mult)
                dve.wait_ge(turned, 2)
                for t in range(2):
                    for h in range(2):
                        nc.vector.tensor_copy(index[:, :, 2 * t + h], bank[2][:, 2 * t + h, 0:n_pair])
                for h in range(2):
                    last = nc.vector.tensor_copy(dst_f[:, :, h], bank[2][:, 2 + h, 0:n_pair])
                last.then_inc(chain, 1)
                dve.wait_ge(chain, 8)
                for h in range(2):
                    nc.vector.tensor_scalar(to_dump[:, :, h], dst_f[:, :, h], -1.0, dump_f[:, h:h + 1],
                                            ALU.mult, ALU.add)
                dve.wait_ge(biased, 1)
                for r in range(2):
                    nc.vector.tensor_copy(c1_row[:, r, :], bank[3][0:1, 0, :])
                for r in range(ROWS):
                    nc.vector.tensor_copy(c2_fill[:, r, :], bank[3][:, 1, :])
                dve.wait_ge(counted, 1)
                nc.vector.tensor_scalar(fast[:, :], bank[4][0:1, 0, 0:1], float(n_pair) - 0.5, None,
                                        ALU.is_ge).then_inc(chain, 1)
                dve.wait_ge(chain, 9)

        def node_rows(table, step):
            if step.last_batch:
                rows = table[N - tail_nodes:N, :].rearrange("(p r) d -> p r d", r=tail_rows)
                return rows, tail_parts, tail_rows
            rows = table[bass.ds(step.batch * BATCH, BATCH), :].rearrange("(p r) d -> p r d", r=ROWS)
            return rows, P, ROWS

        def normalised(step, second):
            lo = 0 if step.dense else 4
            hi = (8 if second else 6) if step.edge else 4
            return lo, hi

        def layer_phase(name, second, fast_plan, slow_plan, fill=False):
            with ExitStack() as scope:
                def psem(what):
                    return scope.enter_context(nc.semaphore(f"{name}_{what}"))

                x_in = [psem(f"x_in{i}") for i in range(UNROLL)]
                edge_in = [psem(f"edge_in{i}") for i in range(UNROLL)]
                side_in = [psem(f"side_in{i}") for i in range(UNROLL)]
                agg_loaded = [psem(f"agg_loaded{i}") for i in range(2)]
                stored = [psem(f"stored{i}") for i in range(2)]
                filled = psem("filled")
                scattered = psem("scattered")
                staged = psem("staged")
                placed = psem("placed")
                same_ready = psem("same_ready")
                same_kept = psem("same_kept")
                stat_link = psem("stat_link")
                mv_ready = psem("mv_ready")
                sd_ready = psem("sd_ready")
                rstd_link = psem("rstd_link")
                coef_ready = psem("coef_ready")
                h_ready = psem("h_ready")
                flipped = psem("flipped")
                hT_ready = psem("hT_ready")
                edge_flipped = psem("edge_flipped")
                eT_ready = psem("eT_ready")
                msg_made = psem("msg_made")
                msg_ready = psem("msg_ready")
                summed = psem("summed")
                sumT_ready = psem("sumT_ready")
                projected = psem("projected")
                edge_out_ready = psem("edge_out_ready")
                node_made = psem("node_made")
                z_link = psem("z_link")
                node_out_ready = psem("node_out_ready")
                idx_link = psem("idx_link")
                pool_passed = psem("pool_passed")

                n_src = 4 if second else 2
                gather_from = x1_dram if second else x
                scatter_to = agg_dram if second else x1_dram

                def both_plans(eng, program):
                    flag = eng.value_load(fast[0:1, 0:1])
                    if slow_plan is None or fast_plan is None:
                        with eng.If(flag != 0 if slow_plan is None else flag == 0):
                            program(slow_plan or fast_plan)
                    else:
                        with eng.If(flag != 0):
                            program(fast_plan)
                        with eng.Else():
                            program(slow_plan)

                block = scope.enter_context(nc.Block())

                @block.sync
                def _(sp):
                    def program(plan):
                        d0, e0 = plan.dense0, plan.edge0

                        def tick(now):
                            ahead = now.at(3)
                            if ahead.dense:
                                if now.at(-1).dense:
                                    sp.wait_ge(node_out_ready, count_before(now, d0))
                                rows, parts, r = node_rows(x1_dram if second else x, ahead)
                                sp.dma_start(X[0:parts, ahead.slot, 0:r, :], rows).then_inc(x_in[ahead.slot], 16)
                            ahead = now.at(2)
                            if ahead.edge and second:
                                if now.at(-2).edge:
                                    sp.wait_ge(edge_flipped, count_before(now.at(-1), e0))
                                if ahead.last_pair:
                                    first = (n_pair - 1) * PAIR
                                    sp.dma_start(attr[:, ahead.slot, 0, :], edge_attr[first:first + P, :])\
                                      .then_inc(side_in[ahead.slot], 16)
                                    sp.dma_start(attr[0:tail_edges - P, ahead.slot, 1, :],
                                                 edge_attr[first + P:E, :]).then_inc(side_in[ahead.slot], 16)
                                else:
                                    rows = edge_attr[bass.ds(ahead.pair * PAIR, PAIR), :]
                                    sp.dma_start(attr[:, ahead.slot, :, :], rows.rearrange("(h e) d -> e h d", h=2))\
                                      .then_inc(side_in[ahead.slot], 16)
                            if ahead.edge and not second:
                                if now.at(-2).edge:
                                    sp.wait_ge(same_ready, count_before(now.at(-1), e0))
                                row = dst_dram[bass.ds(ahead.pair * PAIR, PAIR)].rearrange("(a e) -> a e", a=1)
                                sp.dma_start(dst_row[:, ahead.slot, :], row.partition_broadcast(P))\
                                  .then_inc(side_in[ahead.slot], 16)
                            if now.dense and not second:
                                rows, parts, r = node_rows(agg_dram, now)
                                sp.dma_start(rows, c2_fill[0:parts, 0:r, :]).then_inc(filled, 16)
                            if now.dense:
                                sp.wait_ge(node_out_ready, count_before(now.at(1), d0))
                                rows, parts, r = node_rows(out if second else x1_dram, now)
                                sp.dma_start(rows, node_out[0:parts, now.slot % 2, 0:r, :])\
                                  .then_inc(stored[now.slot % 2], 16)
                            ahead = now.at(1)
                            if ahead.dense and second:
                                if e0 is not None:
                                    reach = plan.dense0 - BAND_ABOVE - 1
                                    done = now.at(1 - reach) if now.at(1 - reach).edge else None
                                    sp.wait_ge(scattered, count_before(now.at(2 - reach), e0, 32) if done
                                               else 32 * n_pair)
                                if now.at(-1).dense:
                                    sp.wait_ge(z_link, count_before(now, d0))
                                rows, parts, r = node_rows(agg_dram, ahead)
                                sp.dma_start(agg_in[0:parts, ahead.slot % 2, 0:r, :], rows)\
                                  .then_inc(agg_loaded[ahead.slot % 2], 16)

                        run_steps(sp, plan, tick)
                        if d0 is not None:
                            for s in range(2):
                                sp.wait_ge(stored[s], 16 * len(range(s, n_batch, 2)))
                            if not second:
                                sp.wait_ge(filled, 16 * n_batch)

                    both_plans(sp, program)

                @block.gpsimd
                def _(pool):
                    def program(plan):
                        d0, e0 = plan.dense0, plan.edge0
                        if e0 is None:
                            return

                        def tick(now):
                            done = now.at(-1)
                            if done.edge:
                                pool.wait_ge(edge_out_ready, count_before(now, e0))
                                pool.wait_ge(placed, count_before(now, e0))
                                if now.at(-2).edge:
                                    pool.wait_ge(scattered, count_before(done, e0, 32))
                                if d0 is not None and not second:
                                    reach = e0 - BAND_ABOVE
                                    whole = done.at(-reach)
                                    if whole.dense:
                                        pool.wait_ge(stored[whole.slot % 2], slot2_uses(whole, d0) * 16)
                                        pool.wait_ge(stored[1 - whole.slot % 2], slot2_uses(whole.at(-1), d0) * 16)
                                    else:
                                        for s in range(2):
                                            pool.wait_ge(stored[s], 16 * len(range(s, n_batch, 2)))
                                pool.sem_inc(pool_passed, 1)
                                for h in range(2):
                                    nc.gpsimd.indirect_dma_start(
                                        out=scatter_to[:, :],
                                        out_offset=bass.IndirectOffsetOnAxis(
                                            ap=scatter_at[:, done.slot, h:h + 1], axis=0),
                                        in_=edge_out[:, done.slot % 2, h, :], in_offset=None,
                                        compute_op=ALU.add).then_inc(scattered, 16)
                            ahead = now.at(2)
                            if ahead.edge:
                                pool.wait_ge(staged, count_before(ahead.at(1), e0))
                                if now.at(-2).edge:
                                    pool.wait_ge(h_ready, count_before(now.at(-1), 0))
                                pool.sem_inc(pool_passed, 1)
                                for c in range(n_src):
                                    nc.gpsimd.indirect_dma_start(
                                        out=X[:, ahead.slot, 4 + c, :], out_offset=None,
                                        in_=gather_from[:, :],
                                        in_offset=bass.IndirectOffsetOnAxis(
                                            ap=gather_at[:, ahead.slot, c:c + 1], axis=0))\
                                        .then_inc(edge_in[ahead.slot], 16)

                        run_steps(pool, plan, tick)
                        pool.wait_ge(scattered, 32 * n_pair)

                    both_plans(pool, program)

                @block.vector
                def _(dve):
                    def program(plan):
                        d0, e0 = plan.dense0, plan.edge0

                        def tick(now):
                            ahead = now.at(3)
                            if ahead.edge:
                                if now.at(-1).edge:
                                    dve.wait_ge(edge_in[ahead.slot], uses_of_slot(now.at(-1), e0) * 16 * n_src)
                                    if second:
                                        dve.wait_ge(scattered, count_before(now, e0, 32))
                                if second:
                                    nc.vector.tensor_copy(scatter_at[:, ahead.slot, :],
                                                          index[:, bass.ds(ahead.pair, 1), 4:6]
                                                          .rearrange("p a c -> p (a c)")).then_inc(placed, 1)
                                nc.vector.tensor_copy(gather_at[:, ahead.slot, 0:n_src],
                                                      index[:, bass.ds(ahead.pair, 1), 0:n_src]
                                                      .rearrange("p a c -> p (a c)")).then_inc(staged, 1)
                            nxt = now.at(1)
                            lo, hi = normalised(nxt, second)
                            q = nxt.slot % 2
                            if nxt.dense or nxt.edge:
                                if nxt.dense:
                                    dve.wait_ge(x_in[nxt.slot], uses_of_slot(nxt, d0) * 16)
                                if nxt.edge:
                                    dve.wait_ge(edge_in[nxt.slot], uses_of_slot(nxt, e0) * 16 * n_src)
                                for t in range(lo, hi):
                                    last = nc.vector.bn_stats(stats[:, q, t, :], X[:, nxt.slot, t, :])
                                last.then_inc(stat_link, 1)
                                dve.wait_ge(stat_link, count_before(nxt, 0, 3) + 1)
                                st = stats[:, q, lo:hi, :]
                                nc.vector.tensor_tensor(gap[:, q, lo:hi], st[:, :, 1], st[:, :, 4], ALU.subtract)
                                nc.vector.tensor_tensor(total[:, q, lo:hi], st[:, :, 1], st[:, :, 4], ALU.add)
                                nc.vector.tensor_tensor(spread[:, q, lo:hi], st[:, :, 2], st[:, :, 5], ALU.add)\
                                    .then_inc(stat_link, 1)
                                dve.wait_ge(stat_link, count_before(nxt, 0, 3) + 2)
                                nc.vector.scalar_tensor_tensor(out=gap[:, q, lo:hi], in0=gap[:, q, lo:hi],
                                                               scalar=P / 4.0, in1=gap[:, q, lo:hi],
                                                               op0=ALU.mult, op1=ALU.mult).then_inc(stat_link, 1)
                                dve.wait_ge(stat_link, count_before(nxt, 0, 3) + 3)
                                nc.vector.tensor_tensor(spread[:, q, lo:hi], spread[:, q, lo:hi],
                                                        gap[:, q, lo:hi], ALU.add).then_inc(mv_ready, 1)
                            if nxt.edge and not second:
                                dve.wait_ge(side_in[nxt.slot], uses_of_slot(nxt, e0) * 16)
                                line = dst_row[:, nxt.slot, :]
                                mine = dst_f[:, bass.ds(nxt.pair, 1), :].rearrange("p a c -> p (a c)")
                                eq = equal[:, q, :]
                                if now.at(-1).edge:
                                    dve.wait_ge(summed, count_before(now, e0))
                                    dve.wait_ge(same_kept, count_before(now, e0))
                                nc.vector.tensor_scalar(eq[:, 0:PAIR], line, mine[:, 0:1], None, ALU.is_equal)
                                nc.vector.tensor_scalar(eq[:, PAIR:], line[:, P:], mine[:, 1:2], None,
                                                        ALU.is_equal).then_inc(same_ready, 1)
                                dve.wait_ge(same_ready, count_before(nxt.at(1), e0))
                                nc.vector.tensor_tensor_reduce(masked, eq[:, 0:PAIR], later[:, :], 1.0, 0.0,
                                                               ALU.mult, ALU.add, n_later[:, q, 0:1])\
                                    .then_inc(idx_link, 1)
                                dve.wait_ge(idx_link, count_before(nxt, e0, 4) + 1)
                                nc.vector.tensor_tensor_reduce(masked[:, 0:P], eq[:, PAIR:], later[:, 0:P], 1.0, 0.0,
                                                               ALU.mult, ALU.add, n_later[:, q, 1:2])\
                                    .then_inc(idx_link, 1)
                                dve.wait_ge(idx_link, count_before(nxt, e0, 4) + 2)
                                away = to_dump[:, bass.ds(nxt.pair, 1), :].rearrange("p a c -> p (a c)")
                                nc.vector.scalar_tensor_tensor(out=moved[:, :], in0=n_later[:, q, :], scalar=1.0,
                                                               in1=away, op0=ALU.min, op1=ALU.mult)\
                                    .then_inc(idx_link, 1)
                                dve.wait_ge(idx_link, count_before(nxt, e0, 4) + 3)
                                if now.at(-3).edge:
                                    dve.wait_ge(scattered, count_before(now.at(-2), e0, 32))
                                nc.vector.tensor_tensor(scatter_at[:, nxt.slot, :], moved[:, :], mine, ALU.add)\
                                    .then_inc(placed, 1)
                                row = index[:, bass.ds(nxt.pair, 1), 4:6].rearrange("p a c -> p (a c)")
                                nc.vector.tensor_tensor(row, moved[:, :], mine, ALU.add).then_inc(idx_link, 1)
                                dve.wait_ge(idx_link, count_before(nxt, e0, 4) + 4)
                            if nxt.dense or nxt.edge:
                                dve.wait_ge(sd_ready, count_before(nxt.at(1), 0))
                                nc.vector.reciprocal(rstd[:, q, lo:hi], sd[:, q, lo:hi]).then_inc(rstd_link, 1)
                                dve.wait_ge(rstd_link, count_before(nxt.at(1), 0))
                                nc.vector.scalar_tensor_tensor(out=nmr[:, q, lo:hi], in0=total[:, q, lo:hi],
                                                               scalar=-0.5, in1=rstd[:, q, lo:hi],
                                                               op0=ALU.mult, op1=ALU.mult).then_inc(coef_ready, 1)
                            w = now.slot % 2
                            if now.dense:
                                dve.wait_ge(node_made, count_before(now.at(1), d0))
                                if now.at(-2).dense:
                                    dve.wait_ge(stored[w], slot2_uses(now.at(-2), d0) * 16)
                            if now.dense and not second:
                                nc.vector.tensor_tensor(node_out[:, w, :, :], bank[4 + w][:, :, :],
                                                        X[:, now.slot, 0:ROWS, :], ALU.add)\
                                    .then_inc(node_out_ready, 1)
                            if now.dense and second:
                                dve.wait_ge(agg_loaded[w], slot2_uses(now, d0) * 16)
                                if now.at(-1).dense:
                                    dve.wait_ge(node_out_ready, count_before(now, d0))
                                nc.vector.tensor_tensor(node_out[:, w, :, :], bank[6][:, :, :], agg_in[:, w, :, :],
                                                        ALU.add).then_inc(z_link, 1)
                                dve.wait_ge(z_link, count_before(now.at(1), d0))
                                nc.vector.scalar_tensor_tensor(out=node_out[:, w, :, :], in0=node_out[:, w, :, :],
                                                               scalar=0.0, in1=X[:, now.slot, 0:ROWS, :],
                                                               op0=ALU.max, op1=ALU.add)\
                                    .then_inc(node_out_ready, 1)
                            if now.edge and second:
                                dve.wait_ge(projected, count_before(now.at(1), e0))
                                if now.at(-2).edge:
                                    dve.wait_ge(scattered, count_before(now.at(-1), e0, 32))
                                nc.vector.tensor_copy(edge_out[:, w, :, :], bank[4][:, 0:2, :])\
                                    .then_inc(edge_out_ready, 1)

                        run_steps(dve, plan, tick)

                    both_plans(dve, program)

                @block.scalar
                def _(act):
                    def program(plan):
                        d0, e0 = plan.dense0, plan.edge0

                        def tick(now):
                            nxt = now.at(1)
                            lo, hi = normalised(nxt, second)
                            q, w = nxt.slot % 2, now.slot % 2

                            def deviation():
                                act.wait_ge(mv_ready, count_before(nxt.at(1), 0))
                                nc.scalar.activation(sd[:, q, lo:hi], spread[:, q, lo:hi], ACT.Sqrt,
                                                     bias=eps_ln[:, :], scale=1.0 / P).then_inc(sd_ready, 1)

                            def normalise(some, last_of_step=False, first_of_step=False):
                                if first_of_step:
                                    act.wait_ge(coef_ready, count_before(nxt.at(1), 0))
                                    if now.at(-1).dense:
                                        act.wait_ge(flipped, count_before(now, d0))
                                    if now.at(-1).edge:
                                        act.wait_ge(edge_flipped if second else summed, count_before(now, e0))
                                for t in some:
                                    last = nc.scalar.activation(H[:, q, t, :], X[:, nxt.slot, t, :], ACT.Relu,
                                                                bias=nmr[:, q, t:t + 1], scale=rstd[:, q, t:t + 1])
                                if last_of_step:
                                    last.then_inc(h_ready, 1)

                            def copy_hT():
                                act.wait_ge(flipped, count_before(now.at(1), d0))
                                if now.at(-1).dense:
                                    act.wait_ge(node_made, count_before(now, d0))
                                nc.scalar.copy(hT[:, :, :], bank[w if not second else 5][:, :, :])\
                                    .then_inc(hT_ready, 1)

                            def copy_sumT():
                                act.wait_ge(summed, count_before(now.at(1), e0))
                                if now.at(-1).edge:
                                    act.wait_ge(projected, count_before(now, e0))
                                nc.scalar.copy(sumT[:, :, :], bank[3 if second else 2][:, 0:2, :])\
                                    .then_inc(sumT_ready, 1)

                            tiles = list(range(lo, hi)) if nxt.dense or nxt.edge else []
                            if not second:
                                if now.edge:
                                    act.wait_ge(same_ready, count_before(now.at(1), e0))
                                    nc.scalar.copy(same[:, bass.ds(now.pair, 1), :].rearrange("p a c -> p (a c)"),
                                                   equal[:, w, :]).then_inc(same_kept, 1)
                                if now.dense:
                                    copy_hT()
                                if now.edge:
                                    copy_sumT()
                                if tiles:
                                    deviation()
                                if now.edge:
                                    act.wait_ge(projected, count_before(now.at(1), e0))
                                    if now.at(-2).edge:
                                        act.wait_ge(scattered, count_before(now.at(-1), e0, 32))
                                    nc.scalar.copy(edge_out[:, w, :, :], bank[3][:, 0:2, :])\
                                        .then_inc(edge_out_ready, 1)
                                if tiles:
                                    normalise(tiles, first_of_step=True, last_of_step=True)
                                return
                            if now.edge:
                                act.wait_ge(edge_flipped, count_before(now.at(1), e0))
                                if now.at(-1).edge:
                                    act.wait_ge(msg_made, count_before(now, e0))
                                nc.scalar.copy(eT[:, 0:4, :], bank[0][:, :, :])
                                nc.scalar.copy(eT[:, 4:6, :], bank[1][:, 0:2, :]).then_inc(eT_ready, 1)
                            if now.dense:
                                copy_hT()
                            if tiles:
                                deviation()
                            if now.edge:
                                act.wait_ge(msg_made, count_before(now.at(1), e0))
                                if now.at(-1).edge:
                                    act.wait_ge(summed, count_before(now, e0))
                                nc.scalar.activation(msg[:, :, :], bank[2][:, 0:2, :], ACT.Relu)\
                                    .then_inc(msg_ready, 1)
                            half = len(tiles) // 2
                            if tiles:
                                normalise(tiles[:half], first_of_step=True)
                            if now.edge:
                                copy_sumT()
                            if tiles:
                                normalise(tiles[half:], last_of_step=True)

                        run_steps(act, plan, tick)

                    both_plans(act, program)

                @block.tensor
                def _(pe):
                    def program(plan):
                        d0, e0 = plan.dense0, plan.edge0

                        def tick(now):
                            w = now.slot % 2

                            def flip_dense():
                                if now.at(-1).dense:
                                    pe.wait_ge(hT_ready, count_before(now, d0))
                                for r in range(ROWS):
                                    last = nc.tensor.transpose(bank[5 if second else w][:, r, :],
                                                               H[:, w, r, :], ident[:, :])
                                last.then_inc(flipped, 1)

                            def sums(lhs, to):
                                if now.at(-1).edge:
                                    pe.wait_ge(sumT_ready, count_before(now, e0))
                                eq = (same[:, bass.ds(now.pair, 1), :].rearrange("p a c -> p (a c)") if second
                                      else equal[:, w, :])
                                nc.tensor.matmul(to[:, 0:2, :].rearrange("p a c -> p (a c)"), lhs[0],
                                                 eq[:, 0:PAIR], start=True, stop=False)
                                nc.tensor.matmul(to[:, 1, :], lhs[1], eq[:, PAIR:], start=False, stop=True)\
                                    .then_inc(summed, 1)

                            def project(weight, to):
                                pe.wait_ge(sumT_ready, count_before(now.at(1), e0))
                                if now.at(-1).edge:
                                    pe.wait_ge(edge_out_ready, count_before(now, e0))
                                for h in range(2):
                                    last = nc.tensor.matmul(to[:, h, :], sumT[:, h, :], weight, start=True, stop=True)
                                last.then_inc(projected, 1)

                            if now.dense or now.edge:
                                pe.wait_ge(h_ready, count_before(now.at(1), 0))
                            if not second:
                                if now.dense:
                                    flip_dense()
                                if now.edge:
                                    pe.wait_ge(same_ready, count_before(now.at(1), e0))
                                    sums([H[:, w, 4, :], H[:, w, 5, :]], bank[2])
                                if now.dense:
                                    if now.at(-2).dense:
                                        pe.wait_ge(node_out_ready, count_before(now.at(-1), d0))
                                    y = bank[4 + w]
                                    nc.tensor.matmul(y[:, :, :].rearrange("p a c -> p (a c)"), ones_row[:, :],
                                                     b0_row.rearrange("p a c -> p (a c)"),
                                                     start=True, stop=False)
                                    pe.wait_ge(hT_ready, count_before(now.at(1), d0))
                                    for r in range(ROWS):
                                        last = nc.tensor.matmul(y[:, r, :], hT[:, r, :], w0_node[:, :],
                                                                start=False, stop=(r == ROWS - 1))
                                    last.then_inc(node_made, 1)
                                if now.edge:
                                    project(w0_edge[:, :], bank[3])
                                return
                            if now.edge:
                                pe.wait_ge(side_in[now.slot], uses_of_slot(now, e0) * 16
                                           + (16 if now.last_pair else 0))
                                if now.at(-1).edge:
                                    pe.wait_ge(eT_ready, count_before(now, e0))
                                for c in range(4):
                                    nc.tensor.transpose(bank[0][:, c, :], H[:, w, 4 + c, :], ident[:, :])
                                for h in range(2):
                                    last = nc.tensor.transpose(bank[1][:, h, :], attr[:, now.slot, h, :], ident[:, :])
                                last.then_inc(edge_flipped, 1)
                            if now.dense:
                                flip_dense()
                            if now.edge:
                                if now.at(-1).edge:
                                    pe.wait_ge(msg_ready, count_before(now, e0))
                                nc.tensor.matmul(bank[2][:, 0:2, :].rearrange("p a c -> p (a c)"), ones_row[:, :],
                                                 c1_row[:, :, :].rearrange("p a c -> p (a c)"),
                                                 start=True, stop=False)
                                pe.wait_ge(eT_ready, count_before(now.at(1), e0))
                                for h in range(2):
                                    for c, block_of_w in ((2, 0), (0, 1), (4, 2)):
                                        last = nc.tensor.matmul(bank[2][:, h, :], eT[:, c + h, :],
                                                                w1T[:, block_of_w, :], start=False,
                                                                stop=(c == 4 and h == 1))
                                last.then_inc(msg_made, 1)
                            if now.dense:
                                if now.at(-1).dense:
                                    pe.wait_ge(z_link, count_before(now, d0))
                                pe.wait_ge(hT_ready, count_before(now.at(1), d0))
                                for r in range(ROWS):
                                    last = nc.tensor.matmul(bank[6][:, r, :], hT[:, r, :], w2T[:, 0, :],
                                                            start=True, stop=True)
                                last.then_inc(node_made, 1)
                            if now.edge:
                                pe.wait_ge(msg_ready, count_before(now.at(1), e0))
                                sums([msg[:, 0, :], msg[:, 1, :]], bank[3])
                                project(w2T[:, 1, :], bank[4])

                        run_steps(pe, plan, tick)

                    both_plans(pe, program)

        def slot2_uses(step, start):
            return uses_in_two(step, start)

        first_lag, second_lag = 4, 5
        layer_phase("nodes1", False, Plan(n_batch, dense0=0, edge0=first_lag), Plan(n_batch, dense0=0))
        layer_phase("edges1", False, None, Plan(n_batch, edge0=0))
        layer_phase("edges2", True, Plan(n_batch, dense0=second_lag, edge0=0), Plan(n_batch, edge0=0))
        layer_phase("nodes2", True, None, Plan(n_batch, dense0=0))


def uses_in_two(step, start):
    per_turn = UNROLL // 2
    first = start + (step.known - start) % 2
    if isinstance(step.turn, int):
        return (step.number - first) // 2 + 1
    return step.turn * per_turn + (step.slot - first) // 2 + 1


_INS = ['x', 'src', 'dst', 'edge_attr_128', 'L0_gnn_W', 'L0_gnn_b', 'L0_gnn_eps', 'L1_gnn_u',
        'L1_gnn_W1', 'L1_gnn_b1', 'L1_gnn_W2', 'L1_gnn_b2']


def kernel(**inputs):
    import numpy as _np
    import concourse.bacc as _bacc
    from concourse import mybir as _mybir
    from concourse.bass_utils import run_bass_kernel_spmd as _run

    nc = _bacc.Bacc("TRN2", target_bir_lowering=False, num_devices=1)
    arrays, args = {}, []
    for name in _INS:
        a = _np.ascontiguousarray(inputs[name])
        arrays[f"in_{name}_dram"] = a
        args.append(nc.dram_tensor(f"in_{name}_dram", a.shape, _mybir.dt.from_np(a.dtype), kind="ExternalInput").ap())
    x = inputs['x']
    out = nc.dram_tensor("out_0_dram", x.shape, _mybir.dt.from_np(_np.dtype('float32')), kind="ExternalOutput").ap()
    gnn_kernel(nc, *args, out)
    r = _run(nc, [arrays], core_ids=[0])
    return r.results[0]["out_0_dram"]
```

```python
from contextlib import ExitStack

import concourse.bass as bass
from concourse import mybir

ALU = mybir.AluOpType
ACT = mybir.ActivationFunctionType
AX = mybir.AxisListType
F32 = mybir.dt.float32
I32 = mybir.dt.int32

P = 128
ROWS = 4
BATCH = P * ROWS
PAIR = 2 * P
UNROLL = 4
BAND_BELOW = 2
BAND_ABOVE = 2
LN_EPS = 1e-5


class Plan:

    def __init__(self, count, dense0=None, edge0=None):
        self.count, self.dense0, self.edge0 = count, dense0, edge0
        ends = [b + count for b in (dense0, edge0) if b is not None]
        self.steps = max(ends)

    def has_dense(self, s):
        return self.dense0 is not None and self.dense0 <= s < self.dense0 + self.count

    def has_edge(self, s):
        return self.edge0 is not None and self.edge0 <= s < self.edge0 + self.count

    def pattern(self, tick, reach):
        near = []
        for s in range(tick - reach, tick + reach + 1):
            near.append((self.has_dense(s), self.has_edge(s),
                         self.dense0 is not None and s == self.dense0 + self.count - 1,
                         self.edge0 is not None and s == self.edge0 + self.count - 1))
        return near


class Step:

    def __init__(self, plan, turn, slot, known):
        self.plan, self.turn, self.slot, self.known = plan, turn, slot, known

    def at(self, offset):
        s = self.slot + offset
        return Step(self.plan, self.turn + s // UNROLL, s % UNROLL, self.known + offset)

    @property
    def number(self):
        return self.turn * UNROLL + self.slot

    @property
    def dense(self):
        return self.plan.has_dense(self.known)

    @property
    def edge(self):
        return self.plan.has_edge(self.known)

    @property
    def batch(self):
        return self.number - self.plan.dense0

    @property
    def pair(self):
        return self.number - self.plan.edge0

    @property
    def last_batch(self):
        return self.known == self.plan.dense0 + self.plan.count - 1

    @property
    def last_pair(self):
        return self.known == self.plan.edge0 + self.plan.count - 1


def count_before(step, start, per=1):
    return (step.number - start) * per


def uses_of_slot(step, start):
    first = start + (step.known - start) % UNROLL
    return (step.number - first) // UNROLL + 1 if isinstance(step.turn, int) else \
        step.turn + (step.slot - first) // UNROLL + 1


def run_steps(eng, plan, body, reach=5):
    tick, end = -reach, plan.steps + reach
    while tick < end:
        run = tick
        while run < end and plan.pattern(run, reach) == plan.pattern(tick, reach):
            run += 1
        start = tick + (-tick) % UNROLL
        turns = max(0, (run - start) // UNROLL)
        if turns >= 2 and tick >= 0:
            for s in range(tick, start):
                body(Step(plan, s // UNROLL, s % UNROLL, s))
            with eng.Fori(start // UNROLL, start // UNROLL + turns) as turn:
                for slot in range(UNROLL):
                    body(Step(plan, turn, slot, start + slot))
            tick = start + UNROLL * turns
        else:
            body(Step(plan, tick // UNROLL, tick % UNROLL, tick))
            tick += 1


def gnn_kernel(nc, x, src, dst, edge_attr, W0, b0, eps, u, W1, b1, W2, b2, out):
    N, D = x.shape
    E = src.shape[0]
    assert D == P
    n_batch = -(-N // BATCH)
    n_pair = -(-E // PAIR)
    assert n_batch == n_pair <= P
    tail_nodes = N - (n_batch - 1) * BATCH
    tail_rows = next(r for r in range(ROWS, 0, -1) if tail_nodes % (16 * r) == 0)
    tail_parts = tail_nodes // tail_rows
    assert tail_parts <= P
    tail_edges = E - (n_pair - 1) * PAIR
    assert P < tail_edges < PAIR
    pad_edges = n_pair * PAIR - E

    x1_dram = nc.dram_tensor("x1_scratch", (N + 2 * P, D), F32, kind="Internal").ap()
    agg_dram = nc.dram_tensor("agg_scratch", (N + 2 * P, D), F32, kind="Internal").ap()
    dst_dram = nc.dram_tensor("dst_padded", (n_pair * PAIR,), I32, kind="Internal").ap()
    src_dram = nc.dram_tensor("src_padded", (n_pair * PAIR,), I32, kind="Internal").ap()

    with ExitStack() as ctx:
        def sb(name, shape, dt=F32):
            return ctx.enter_context(nc.sbuf_tensor(name, shape, dt))

        def sem(name):
            return ctx.enter_context(nc.semaphore(name))

        ident = sb("ident", [P, P])
        later = sb("later", [P, PAIR])
        ones_row = sb("ones_row", [1, P])
        w0_node = sb("w0_node", [P, P])
        w0_edge = sb("w0_edge", [P, P])
        w1T = sb("w1T", [P, 4, P])
        w2T = sb("w2T", [P, 3, P])
        c1_row = sb("c1_row", [1, 2, P])
        c2_fill = sb("c2_fill", [P, ROWS, P])
        eps_ln = sb("eps_ln", [P, 1])
        dst_f = sb("dst_f", [P, n_pair, 2])
        to_dump = sb("to_dump", [P, n_pair, 2])
        index = sb("index", [P, n_pair, 6], I32)
        same = sb("same", [P, n_pair, 3 * P])
        fast = sb("fast", [1, 1], I32)

        X = sb("X", [P, UNROLL, 8, P])
        H = sb("H", [P, 2, 8, P])
        stats = sb("stats", [P, 2, 8, 6])
        total = sb("total", [P, 2, 8])
        gap = sb("gap", [P, 2, 8])
        spread = sb("spread", [P, 2, 8])
        sd = sb("sd", [P, 2, 8])
        rstd = sb("rstd", [P, 2, 8])
        nmr = sb("nmr", [P, 2, 8])
        hT = sb("hT", [P, ROWS, P])
        eT = sb("eT", [P, 6, P])
        sumT = sb("sumT", [P, 2, P])
        msg = sb("msg", [P, 2, P])
        edge_out = sb("edge_out", [P, 2, 2, P])
        node_out = sb("node_out", [P, 2, ROWS, P])
        agg_in = sb("agg_in", [P, 2, ROWS, P])
        attr = sb("attr", [P, UNROLL, 2, P])
        dst_row = attr[:, :, :, :].rearrange("p s h d -> p s (h d)").bitcast(I32)
        b0_row = agg_in[0:1, 0, :, :]
        masked = agg_in[:, 1, 0:2, :].rearrange("p a c -> p (a c)")
        n_later = sb("n_later", [P, 2, 2])
        moved = sb("moved", [P, 2])
        gather_at = sb("gather_at", [P, UNROLL, 4], I32)
        scatter_at = sb("scatter_at", [P, UNROLL, 2], I32)

        bank = [ctx.enter_context(nc.psum_tensor(f"bank{i}", [P, 4, P], F32)) for i in range(8)]

        w1_in, w2_in = hT, eT
        pair_i = [X[0:n_pair, 0, 0:2, :].bitcast(I32), X[0:n_pair, 0, 2:4, :].bitcast(I32)]
        pair_f = [X[0:n_pair, 1, 0:2, :], X[0:n_pair, 1, 2:4, :]]
        equal = eT[:, :, :].rearrange("p (q c) d -> p q (c d)", q=2)
        u_col = sb("u_col", [P, 1])
        u_wide = H[:, 0, 0, :]
        eps_col = sb("eps_col", [P, 1])
        brow = H[0:1, 1, 0:2, :]
        pad_dst = sb("pad_dst", [1, pad_edges], I32)
        pad_src = sb("pad_src", [1, pad_edges], I32)
        dump_i = sb("dump_i", [P, 2], I32)
        dump_f = sb("dump_f", [P, 2])
        base_i = sb("base_i", [P, 1], I32)
        base_f = sb("base_f", [P, 1])
        bound = sb("bound", [P, 4])
        ok = sb("ok", [P, 1])
        ones_col = sb("ones_col", [P, 1])
        zero_row = H[:, 0, 1, :]

        with ExitStack() as setup:
            def ssem(name):
                return ctx.enter_context(nc.semaphore(name))

            weights_in = ssem("weights_in")
            rows_in = ssem("rows_in")
            pads_ready = ssem("pads_ready")
            padded = ssem("padded")
            pairs_in = ssem("pairs_in")
            dump_zeroed = ssem("dump_zeroed")
            consts = ssem("consts")
            dve_consts = ssem("dve_consts")
            pairs_f = ssem("pairs_f")
            turned = ssem("turned")
            w_ready = ssem("w_ready")
            biased = ssem("biased")
            chain = ssem("chain")
            counted = ssem("counted")
            block = setup.enter_context(nc.Block())

            @block.sync
            def _(sp):
                sp.dma_start(w1_in[:, :, :], W1.rearrange("o (c k) -> o c k", c=4)).then_inc(weights_in, 16)
                sp.dma_start(w2_in[:, 0:3, :], W2.rearrange("o (c k) -> o c k", c=3)).then_inc(weights_in, 16)
                sp.dma_start(w0_edge[:, :], W0).then_inc(weights_in, 16)
                with nc.allow_non_contiguous_dma(reason="one vector, a number to a partition"):
                    sp.dma_start(u_col[:, :], u[0:1, :].rearrange("a d -> d a")).then_inc(weights_in, 16)
                sp.dma_start(eps_col[:, :], eps.rearrange("(a d) -> a d", a=1).partition_broadcast(P)).then_inc(weights_in, 16)
                for r in range(ROWS):
                    sp.dma_start(b0_row[:, r, :], b0.rearrange("(a d) -> a d", a=1)).then_inc(rows_in, 16)
                sp.dma_start(brow[:, 0, :], b1.rearrange("(a d) -> a d", a=1)).then_inc(rows_in, 16)
                sp.dma_start(brow[:, 1, :], b2.rearrange("(a d) -> a d", a=1)).then_inc(rows_in, 16)
                sp.dma_start(dst_dram[0:E], dst).then_inc(padded, 16)
                sp.dma_start(src_dram[0:E], src).then_inc(padded, 16)
                sp.wait_ge(pads_ready, 2)
                sp.dma_start(dst_dram[E:n_pair * PAIR], pad_dst[0:1, :]).then_inc(padded, 16)
                sp.dma_start(src_dram[E:n_pair * PAIR], pad_src[0:1, :]).then_inc(padded, 16)
                sp.wait_ge(padded, 64)
                for t, of in enumerate((src_dram, dst_dram)):
                    sp.dma_start(pair_i[t], of.rearrange("(q h e) -> q h e", h=2, e=P)).then_inc(pairs_in, 16)
                sp.wait_ge(dve_consts, 4)
                for h in range(2):
                    sp.dma_start(x1_dram[N + h * P:N + (h + 1) * P, :], zero_row).then_inc(dump_zeroed, 16)
                for h in range(2):
                    sp.dma_start(agg_dram[N + h * P:N + (h + 1) * P, :], zero_row).then_inc(dump_zeroed, 16)
                sp.wait_ge(dump_zeroed, 64)

            @block.gpsimd
            def _(pool):
                nc.gpsimd.iota(pad_dst[:, :], pattern=[[1, pad_edges]], base=N + 2 * P - pad_edges,
                               channel_multiplier=0).then_inc(pads_ready, 1)
                nc.gpsimd.memset(pad_src[:, :], 0).then_inc(pads_ready, 1)
                nc.gpsimd.iota(dump_i[:, :], pattern=[[P, 2]], base=N, channel_multiplier=1).then_inc(consts, 1)
                nc.gpsimd.iota(base_i[:, :], pattern=[[0, 1]], base=0, channel_multiplier=BATCH).then_inc(consts, 1)
                pool.wait_ge(dve_consts, 2)
                nc.gpsimd.affine_select(out=ident[:, :], in_=ident[:, :], compare_op=ALU.not_equal, fill=1.0,
                                        base=0, pattern=[[-1, P]], channel_multiplier=1).then_inc(consts, 1)
                nc.gpsimd.affine_select(out=later[:, :], in_=later[:, :], compare_op=ALU.is_gt, fill=0.0,
                                        base=0, pattern=[[1, PAIR]], channel_multiplier=-1).then_inc(consts, 1)

            @block.tensor
            def _(pe):
                pe.wait_ge(consts, 4)
                pe.wait_ge(weights_in, 80)
                for c in range(4):
                    nc.tensor.transpose(bank[0][:, c, :], w1_in[:, c, :], ident[:, :])
                for c in range(3):
                    last = nc.tensor.transpose(bank[1][:, c, :], w2_in[:, c, :], ident[:, :])
                last.then_inc(turned, 1)
                pe.wait_ge(pairs_f, 2)
                for t in range(2):
                    for h in range(2):
                        last = nc.tensor.transpose(bank[2][:, 2 * t + h, 0:n_pair], pair_f[t][:, h, :],
                                                   ident[0:n_pair, 0:n_pair])
                last.then_inc(turned, 1)
                pe.wait_ge(w_ready, 3)
                pe.wait_ge(rows_in, 16 * (ROWS + 2))
                pe.wait_ge(dve_consts, 5)
                for c, wu in enumerate((w1T[:, 3, :], w2T[:, 2, :])):
                    nc.tensor.matmul(bank[3][:, c, :], u_wide, wu, start=True, stop=False)
                    last = nc.tensor.matmul(bank[3][:, c, :], ones_row[:, :], brow[:, c, :], start=False, stop=True)
                last.then_inc(biased, 1)
                pe.wait_ge(chain, 6)
                nc.tensor.matmul(bank[4][0:1, 0, 0:1], ok[0:n_pair, :], ones_col[0:n_pair, :],
                                 start=True, stop=True).then_inc(counted, 1)

            @block.vector
            def _(dve):
                nc.vector.memset(ident[:, :], 0.0).then_inc(dve_consts, 1)
                nc.vector.memset(later[:, :], 1.0).then_inc(dve_consts, 1)
                nc.vector.memset(ones_col[:, :], 1.0).then_inc(dve_consts, 1)
                nc.vector.memset(zero_row, 0.0).then_inc(dve_consts, 1)
                nc.vector.memset(ones_row[:, :], 1.0).then_inc(dve_consts, 1)
                nc.vector.memset(eps_ln[:, :], LN_EPS).then_inc(dve_consts, 1)
                dve.wait_ge(pairs_in, 32)
                for t in range(2):
                    nc.vector.tensor_copy(pair_f[t], pair_i[t]).then_inc(pairs_f, 1)
                dve.wait_ge(consts, 4)
                nc.vector.tensor_copy(dump_f[:, :], dump_i[:, :]).then_inc(chain, 1)
                nc.vector.tensor_copy(base_f[:, :], base_i[:, :]).then_inc(chain, 1)
                dve.wait_ge(pairs_f, 2)
                nc.vector.tensor_reduce(bound[0:n_pair, 0:1], pair_f[1], AX.XY, ALU.max).then_inc(chain, 1)
                nc.vector.tensor_reduce(bound[0:n_pair, 1:2], pair_f[1], AX.XY, ALU.min).then_inc(chain, 1)
                dve.wait_ge(chain, 4)
                nc.vector.tensor_scalar(bound[0:n_pair, 2:3], bound[0:n_pair, 0:1], base_f[0:n_pair, :],
                                        float((BAND_ABOVE + 1) * BATCH), ALU.subtract, ALU.is_lt).then_inc(chain, 1)
                dve.wait_ge(chain, 5)
                nc.vector.tensor_scalar(bound[0:n_pair, 3:4], bound[0:n_pair, 1:2], base_f[0:n_pair, :],
                                        float(-BAND_BELOW * BATCH), ALU.subtract, ALU.is_ge).then_inc(w_ready, 1)
                dve.wait_ge(w_ready, 1)
                nc.vector.tensor_tensor(ok[0:n_pair, :], bound[0:n_pair, 2:3], bound[0:n_pair, 3:4],
                                        ALU.mult).then_inc(chain, 1)
                dve.wait_ge(weights_in, 80)
                nc.vector.tensor_scalar(u_wide, zero_row, u_col[:, :], None, ALU.add).then_inc(w_ready, 1)
                nc.vector.tensor_scalar(eps_col[:, :], eps_col[:, :], 1.0, None, ALU.add).then_inc(chain, 1)
                dve.wait_ge(turned, 1)
                nc.vector.tensor_copy(w1T[:, :, :], bank[0][:, :, :])
                nc.vector.tensor_copy(w2T[:, :, :], bank[1][:, 0:3, :]).then_inc(w_ready, 1)
                dve.wait_ge(chain, 7)
                nc.vector.tensor_scalar(w0_node[:, :], w0_edge[:, :], eps_col[:, :], None, ALU.mult)
                dve.wait_ge(turned, 2)
                for t in range(2):
                    for h in range(2):
                        nc.vector.tensor_copy(index[:, :, 2 * t + h], bank[2][:, 2 * t + h, 0:n_pair])
                for h in range(2):
                    last = nc.vector.tensor_copy(dst_f[:, :, h], bank[2][:, 2 + h, 0:n_pair])
                last.then_inc(chain, 1)
                dve.wait_ge(chain, 8)
                for h in range(2):
                    nc.vector.tensor_scalar(to_dump[:, :, h], dst_f[:, :, h], -1.0, dump_f[:, h:h + 1],
                                            ALU.mult, ALU.add)
                dve.wait_ge(biased, 1)
                for r in range(2):
                    nc.vector.tensor_copy(c1_row[:, r, :], bank[3][0:1, 0, :])
                for r in range(ROWS):
                    nc.vector.tensor_copy(c2_fill[:, r, :], bank[3][:, 1, :])
                dve.wait_ge(counted, 1)
                nc.vector.tensor_scalar(fast[:, :], bank[4][0:1, 0, 0:1], float(n_pair) - 0.5, None,
                                        ALU.is_ge).then_inc(chain, 1)
                dve.wait_ge(chain, 9)

        def node_rows(table, step):
            if step.last_batch:
                rows = table[N - tail_nodes:N, :].rearrange("(p r) d -> p r d", r=tail_rows)
                return rows, tail_parts, tail_rows
            rows = table[bass.ds(step.batch * BATCH, BATCH), :].rearrange("(p r) d -> p r d", r=ROWS)
            return rows, P, ROWS

        def normalised(step, second):
            lo = 0 if step.dense else 4
            hi = (8 if second else 6) if step.edge else 4
            return lo, hi

        semaphores = {}

        def layer_phase(name, second, fast_plan, slow_plan, fill=False):
            with ExitStack() as scope:
                def psem(what, of=None):
                    key = f"{of or layer}_{what}"
                    if key not in semaphores:
                        semaphores[key] = ctx.enter_context(nc.semaphore(key))
                    return semaphores[key]

                layer = "second" if second else "first"

                x_in = [psem(f"x_in{i}") for i in range(UNROLL)]
                edge_in = [psem(f"edge_in{i}") for i in range(UNROLL)]
                side_in = [psem(f"side_in{i}") for i in range(UNROLL)]
                agg_loaded = [psem(f"agg_loaded{i}") for i in range(2)]
                stored = [psem(f"stored{i}") for i in range(2)]
                filled = psem("filled")
                scattered = psem("scattered")
                staged = psem("staged")
                placed = psem("placed")
                same_ready = psem("same_ready")
                same_kept = psem("same_kept")
                stat_link = psem("stat_link", name)
                mv_ready = psem("mv_ready", name)
                sd_ready = psem("sd_ready", name)
                rstd_link = psem("rstd_link", name)
                coef_ready = psem("coef_ready", name)
                h_ready = psem("h_ready", name)
                flipped = psem("flipped")
                hT_ready = psem("hT_ready")
                edge_flipped = psem("edge_flipped")
                eT_ready = psem("eT_ready")
                msg_made = psem("msg_made")
                msg_ready = psem("msg_ready")
                summed = psem("summed")
                sumT_ready = psem("sumT_ready")
                projected = psem("projected")
                edge_out_ready = psem("edge_out_ready")
                node_made = psem("node_made")
                z_link = psem("z_link")
                node_out_ready = psem("node_out_ready")
                idx_link = psem("idx_link")
                pool_passed = psem("pool_passed")

                n_src = 4 if second else 2
                gather_from = x1_dram if second else x
                scatter_to = agg_dram if second else x1_dram

                def both_plans(eng, program):
                    flag = eng.value_load(fast[0:1, 0:1])
                    if slow_plan is None or fast_plan is None:
                        with eng.If(flag != 0 if slow_plan is None else flag == 0):
                            program(slow_plan or fast_plan)
                    else:
                        with eng.If(flag != 0):
                            program(fast_plan)
                        with eng.Else():
                            program(slow_plan)

                block = scope.enter_context(nc.Block())

                @block.sync
                def _(sp):
                    def program(plan):
                        d0, e0 = plan.dense0, plan.edge0

                        def tick(now):
                            ahead = now.at(3)
                            if ahead.dense:
                                if now.at(-1).dense:
                                    sp.wait_ge(node_out_ready, count_before(now, d0))
                                rows, parts, r = node_rows(x1_dram if second else x, ahead)
                                sp.dma_start(X[0:parts, ahead.slot, 0:r, :], rows).then_inc(x_in[ahead.slot], 16)
                            ahead = now.at(2)
                            if ahead.edge and second:
                                if now.at(-2).edge:
                                    sp.wait_ge(edge_flipped, count_before(now.at(-1), e0))
                                if ahead.last_pair:
                                    first = (n_pair - 1) * PAIR
                                    sp.dma_start(attr[:, ahead.slot, 0, :], edge_attr[first:first + P, :])\
                                      .then_inc(side_in[ahead.slot], 16)
                                    sp.dma_start(attr[0:tail_edges - P, ahead.slot, 1, :],
                                                 edge_attr[first + P:E, :]).then_inc(side_in[ahead.slot], 16)
                                else:
                                    rows = edge_attr[bass.ds(ahead.pair * PAIR, PAIR), :]
                                    sp.dma_start(attr[:, ahead.slot, :, :], rows.rearrange("(h e) d -> e h d", h=2))\
                                      .then_inc(side_in[ahead.slot], 16)
                            if ahead.edge and not second:
                                if now.at(-2).edge:
                                    sp.wait_ge(same_ready, count_before(now.at(-1), e0))
                                row = dst_dram[bass.ds(ahead.pair * PAIR, PAIR)].rearrange("(a e) -> a e", a=1)
                                sp.dma_start(dst_row[:, ahead.slot, :], row.partition_broadcast(P))\
                                  .then_inc(side_in[ahead.slot], 16)
                            if now.dense and not second:
                                rows, parts, r = node_rows(agg_dram, now)
                                sp.dma_start(rows, c2_fill[0:parts, 0:r, :]).then_inc(filled, 16)
                            done = now.at(-1)
                            if done.dense:
                                sp.wait_ge(node_out_ready, count_before(now, d0))
                                rows, parts, r = node_rows(out if second else x1_dram, done)
                                sp.dma_start(rows, node_out[0:parts, done.slot % 2, 0:r, :])\
                                  .then_inc(stored[done.slot % 2], 16)
                            if now.dense and second:
                                if e0 is not None:
                                    last_pair = now.at(BAND_ABOVE - d0 + e0)
                                    sp.wait_ge(scattered, count_before(last_pair.at(1), e0, 32) if last_pair.edge
                                               else 32 * n_pair)
                                if now.at(-2).dense:
                                    sp.wait_ge(z_link, count_before(now.at(-1), d0))
                                rows, parts, r = node_rows(agg_dram, now)
                                sp.dma_start(agg_in[0:parts, now.slot % 2, 0:r, :], rows)\
                                  .then_inc(agg_loaded[now.slot % 2], 16)

                        run_steps(sp, plan, tick)
                        if d0 is not None:
                            for s in range(2):
                                sp.wait_ge(stored[s], 16 * len(range(s, n_batch, 2)))
                            if not second:
                                sp.wait_ge(filled, 16 * n_batch)

                    both_plans(sp, program)

                @block.gpsimd
                def _(pool):
                    def program(plan):
                        d0, e0 = plan.dense0, plan.edge0
                        if e0 is None:
                            return

                        def tick(now):
                            done = now.at(-3 if second else -2)
                            if done.edge:
                                pool.wait_ge(edge_out_ready, count_before(done.at(1), e0))
                                pool.wait_ge(placed, count_before(done.at(1), e0))
                                if done.at(-1).edge:
                                    pool.wait_ge(scattered, count_before(done, e0, 32))
                                if d0 is not None and not second:
                                    reach = e0 - BAND_ABOVE
                                    whole = done.at(-reach)
                                    if whole.dense:
                                        pool.wait_ge(stored[whole.slot % 2], slot2_uses(whole, d0) * 16)
                                        pool.wait_ge(stored[1 - whole.slot % 2], slot2_uses(whole.at(-1), d0) * 16)
                                    else:
                                        for s in range(2):
                                            pool.wait_ge(stored[s], 16 * len(range(s, n_batch, 2)))
                                pool.sem_inc(pool_passed, 1)
                                for h in range(2):
                                    nc.gpsimd.indirect_dma_start(
                                        out=scatter_to[:, :],
                                        out_offset=bass.IndirectOffsetOnAxis(
                                            ap=scatter_at[:, done.slot, h:h + 1], axis=0),
                                        in_=edge_out[:, done.slot % 2, h, :], in_offset=None,
                                        compute_op=ALU.add).then_inc(scattered, 16)
                            ahead = now.at(3)
                            if ahead.edge:
                                pool.wait_ge(staged, count_before(ahead.at(1), e0))
                                if now.at(-1).edge:
                                    pool.wait_ge(h_ready, count_before(now, 0))
                                pool.sem_inc(pool_passed, 1)
                                for c in range(n_src):
                                    nc.gpsimd.indirect_dma_start(
                                        out=X[:, ahead.slot, 4 + c, :], out_offset=None,
                                        in_=gather_from[:, :],
                                        in_offset=bass.IndirectOffsetOnAxis(
                                            ap=gather_at[:, ahead.slot, c:c + 1], axis=0))\
                                        .then_inc(edge_in[ahead.slot], 16)

                        run_steps(pool, plan, tick)
                        pool.wait_ge(scattered, 32 * n_pair)

                    both_plans(pool, program)

                @block.vector
                def _(dve):
                    def program(plan):
                        d0, e0 = plan.dense0, plan.edge0

                        def tick(now):
                            done = now.at(-1)
                            w = done.slot % 2
                            if done.dense:
                                dve.wait_ge(node_made, count_before(now, d0))
                                if now.at(-3).dense:
                                    dve.wait_ge(stored[w], slot2_uses(now.at(-3), d0) * 16)
                            if done.dense and not second:
                                nc.vector.tensor_tensor(node_out[:, w, :, :], bank[4 + w][:, :, :],
                                                        X[:, done.slot, 0:ROWS, :], ALU.add)\
                                    .then_inc(node_out_ready, 1)
                            if done.dense and second:
                                dve.wait_ge(agg_loaded[w], slot2_uses(done, d0) * 16)
                                nc.vector.tensor_tensor(node_out[:, w, :, :], bank[6][:, :, :], agg_in[:, w, :, :],
                                                        ALU.add).then_inc(z_link, 1)
                                dve.wait_ge(z_link, count_before(now, d0))
                                nc.vector.scalar_tensor_tensor(out=node_out[:, w, :, :], in0=node_out[:, w, :, :],
                                                               scalar=0.0, in1=X[:, done.slot, 0:ROWS, :],
                                                               op0=ALU.max, op1=ALU.add)\
                                    .then_inc(node_out_ready, 1)
                            older = now.at(-2)
                            if older.edge and second:
                                dve.wait_ge(projected, count_before(now.at(-1), e0))
                                if now.at(-4).edge:
                                    dve.wait_ge(scattered, count_before(now.at(-3), e0, 32))
                                nc.vector.tensor_copy(edge_out[:, older.slot % 2, :, :], bank[4][:, 0:2, :])\
                                    .then_inc(edge_out_ready, 1)
                            if done.edge and second:
                                if now.at(-5).edge:
                                    dve.wait_ge(scattered, count_before(now.at(-4), e0, 32))
                                nc.vector.tensor_copy(scatter_at[:, done.slot, :],
                                                      index[:, bass.ds(done.pair, 1), 4:6]
                                                      .rearrange("p a c -> p (a c)")).then_inc(placed, 1)
                            ahead = now.at(4)
                            if ahead.edge:
                                if now.edge:
                                    dve.wait_ge(edge_in[ahead.slot], uses_of_slot(now, e0) * 16 * n_src)
                                nc.vector.tensor_copy(gather_at[:, ahead.slot, 0:n_src],
                                                      index[:, bass.ds(ahead.pair, 1), 0:n_src]
                                                      .rearrange("p a c -> p (a c)")).then_inc(staged, 1)
                            nxt = now.at(2)
                            lo, hi = normalised(nxt, second)
                            q = nxt.slot % 2
                            if nxt.dense or nxt.edge:
                                if nxt.dense:
                                    dve.wait_ge(x_in[nxt.slot], uses_of_slot(nxt, d0) * 16)
                                if nxt.edge:
                                    dve.wait_ge(edge_in[nxt.slot], uses_of_slot(nxt, e0) * 16 * n_src)
                                for t in range(lo, hi):
                                    last = nc.vector.bn_stats(stats[:, q, t, :], X[:, nxt.slot, t, :])
                                last.then_inc(stat_link, 1)
                                dve.wait_ge(stat_link, count_before(nxt, 0, 3) + 1)
                                st = stats[:, q, lo:hi, :]
                                nc.vector.tensor_tensor(gap[:, q, lo:hi], st[:, :, 1], st[:, :, 4], ALU.subtract)
                                nc.vector.tensor_tensor(total[:, q, lo:hi], st[:, :, 1], st[:, :, 4], ALU.add)
                                nc.vector.tensor_tensor(spread[:, q, lo:hi], st[:, :, 2], st[:, :, 5], ALU.add)\
                                    .then_inc(stat_link, 1)
                                dve.wait_ge(stat_link, count_before(nxt, 0, 3) + 2)
                                nc.vector.scalar_tensor_tensor(out=gap[:, q, lo:hi], in0=gap[:, q, lo:hi],
                                                               scalar=P / 4.0, in1=gap[:, q, lo:hi],
                                                               op0=ALU.mult, op1=ALU.mult).then_inc(stat_link, 1)
                                dve.wait_ge(stat_link, count_before(nxt, 0, 3) + 3)
                                nc.vector.tensor_tensor(spread[:, q, lo:hi], spread[:, q, lo:hi],
                                                        gap[:, q, lo:hi], ALU.add).then_inc(mv_ready, 1)
                            nxt = now.at(1)
                            q = nxt.slot % 2
                            if nxt.edge and not second:
                                dve.wait_ge(side_in[nxt.slot], uses_of_slot(nxt, e0) * 16)
                                line = dst_row[:, nxt.slot, :]
                                mine = dst_f[:, bass.ds(nxt.pair, 1), :].rearrange("p a c -> p (a c)")
                                eq = equal[:, q, :]
                                if now.at(-1).edge:
                                    dve.wait_ge(summed, count_before(now, e0))
                                    dve.wait_ge(same_kept, count_before(now, e0))
                                nc.vector.tensor_scalar(eq[:, 0:PAIR], line, mine[:, 0:1], None, ALU.is_equal)
                                nc.vector.tensor_scalar(eq[:, PAIR:], line[:, P:], mine[:, 1:2], None,
                                                        ALU.is_equal).then_inc(same_ready, 1)
                                dve.wait_ge(same_ready, count_before(nxt.at(1), e0))
                                nc.vector.tensor_tensor_reduce(masked, eq[:, 0:PAIR], later[:, :], 1.0, 0.0,
                                                               ALU.mult, ALU.add, n_later[:, q, 0:1])\
                                    .then_inc(idx_link, 1)
                                dve.wait_ge(idx_link, count_before(nxt, e0, 4) + 1)
                                nc.vector.tensor_tensor_reduce(masked[:, 0:P], eq[:, PAIR:], later[:, 0:P], 1.0, 0.0,
                                                               ALU.mult, ALU.add, n_later[:, q, 1:2])\
                                    .then_inc(idx_link, 1)
                                dve.wait_ge(idx_link, count_before(nxt, e0, 4) + 2)
                                away = to_dump[:, bass.ds(nxt.pair, 1), :].rearrange("p a c -> p (a c)")
                                nc.vector.scalar_tensor_tensor(out=moved[:, :], in0=n_later[:, q, :], scalar=1.0,
                                                               in1=away, op0=ALU.min, op1=ALU.mult)\
                                    .then_inc(idx_link, 1)
                                dve.wait_ge(idx_link, count_before(nxt, e0, 4) + 3)
                                if now.at(-3).edge:
                                    dve.wait_ge(scattered, count_before(now.at(-2), e0, 32))
                                nc.vector.tensor_tensor(scatter_at[:, nxt.slot, :], moved[:, :], mine, ALU.add)\
                                    .then_inc(placed, 1)
                                row = index[:, bass.ds(nxt.pair, 1), 4:6].rearrange("p a c -> p (a c)")
                                nc.vector.tensor_tensor(row, moved[:, :], mine, ALU.add).then_inc(idx_link, 1)
                                dve.wait_ge(idx_link, count_before(nxt, e0, 4) + 4)
                            nxt = now.at(2)
                            q = nxt.slot % 2
                            if nxt.dense or nxt.edge:
                                dve.wait_ge(sd_ready, count_before(nxt.at(1), 0))
                                nc.vector.reciprocal(rstd[:, q, lo:hi], sd[:, q, lo:hi]).then_inc(rstd_link, 1)
                                dve.wait_ge(rstd_link, count_before(nxt.at(1), 0))
                                nc.vector.scalar_tensor_tensor(out=nmr[:, q, lo:hi], in0=total[:, q, lo:hi],
                                                               scalar=-0.5, in1=rstd[:, q, lo:hi],
                                                               op0=ALU.mult, op1=ALU.mult).then_inc(coef_ready, 1)
                        run_steps(dve, plan, tick)

                    both_plans(dve, program)

                @block.scalar
                def _(act):
                    def program(plan):
                        d0, e0 = plan.dense0, plan.edge0

                        def tick(now):
                            nxt, later_step = now.at(1), now.at(2)
                            w = now.slot % 2

                            def deviation():
                                lo, hi = normalised(later_step, second)
                                r = later_step.slot % 2
                                act.wait_ge(mv_ready, count_before(now.at(3), 0))
                                nc.scalar.activation(sd[:, r, lo:hi], spread[:, r, lo:hi], ACT.Sqrt,
                                                     bias=eps_ln[:, :], scale=1.0 / P).then_inc(sd_ready, 1)

                            def normalise(part, parts):
                                if not (nxt.dense or nxt.edge):
                                    return
                                lo, hi = normalised(nxt, second)
                                q = nxt.slot % 2
                                if part == 0:
                                    act.wait_ge(coef_ready, count_before(nxt.at(1), 0))
                                    if now.at(-1).dense:
                                        act.wait_ge(flipped, count_before(now, d0))
                                    if now.at(-1).edge:
                                        act.wait_ge(edge_flipped if second else summed, count_before(now, e0))
                                for t in range(lo + (hi - lo) * part // parts, lo + (hi - lo) * (part + 1) // parts):
                                    last = nc.scalar.activation(H[:, q, t, :], X[:, nxt.slot, t, :], ACT.Relu,
                                                                bias=nmr[:, q, t:t + 1], scale=rstd[:, q, t:t + 1])
                                if part == parts - 1:
                                    last.then_inc(h_ready, 1)

                            def copy_hT():
                                act.wait_ge(flipped, count_before(now.at(1), d0))
                                if now.at(-1).dense:
                                    act.wait_ge(node_made, count_before(now, d0))
                                nc.scalar.copy(hT[:, :, :], bank[w if not second else 5][:, :, :])\
                                    .then_inc(hT_ready, 1)

                            def copy_sumT(of):
                                act.wait_ge(summed, count_before(of.at(1), e0))
                                if of.at(-1).edge:
                                    act.wait_ge(projected, count_before(of, e0))
                                nc.scalar.copy(sumT[:, :, :], bank[3 if second else 2][:, 0:2, :])\
                                    .then_inc(sumT_ready, 1)

                            done = now.at(-1)
                            if not second:
                                normalise(0, 2)
                                if now.dense:
                                    copy_hT()
                                normalise(1, 2)
                                if now.edge:
                                    copy_sumT(now)
                                if done.edge:
                                    act.wait_ge(projected, count_before(now, e0))
                                    if now.at(-3).edge:
                                        act.wait_ge(scattered, count_before(now.at(-2), e0, 32))
                                    nc.scalar.copy(edge_out[:, done.slot % 2, :, :], bank[3][:, 0:2, :])\
                                        .then_inc(edge_out_ready, 1)
                                if now.edge:
                                    act.wait_ge(same_ready, count_before(now.at(1), e0))
                                    nc.scalar.copy(same[:, bass.ds(now.pair, 1), :].rearrange("p a c -> p (a c)"),
                                                   equal[:, w, :]).then_inc(same_kept, 1)
                                if later_step.dense or later_step.edge:
                                    deviation()
                                return
                            normalise(0, 3)
                            if now.edge:
                                act.wait_ge(edge_flipped, count_before(now.at(1), e0))
                                if now.at(-1).edge:
                                    act.wait_ge(msg_made, count_before(now, e0))
                                nc.scalar.copy(eT[:, 0:4, :], bank[0][:, :, :])
                                nc.scalar.copy(eT[:, 4:6, :], bank[1][:, 0:2, :]).then_inc(eT_ready, 1)
                            if now.dense:
                                copy_hT()
                            normalise(1, 3)
                            if done.edge:
                                copy_sumT(done)
                            normalise(2, 3)
                            if later_step.dense or later_step.edge:
                                deviation()
                            if now.edge:
                                act.wait_ge(msg_made, count_before(now.at(1), e0))
                                if now.at(-1).edge:
                                    act.wait_ge(summed, count_before(now, e0))
                                nc.scalar.activation(msg[:, :, :], bank[2][:, 0:2, :], ACT.Relu)\
                                    .then_inc(msg_ready, 1)

                        run_steps(act, plan, tick)

                    both_plans(act, program)

                @block.tensor
                def _(pe):
                    def program(plan):
                        d0, e0 = plan.dense0, plan.edge0

                        def tick(now):
                            w = now.slot % 2

                            def flip_dense():
                                if now.at(-1).dense:
                                    pe.wait_ge(hT_ready, count_before(now, d0))
                                for r in range(ROWS):
                                    last = nc.tensor.transpose(bank[5 if second else w][:, r, :],
                                                               H[:, w, r, :], ident[:, :])
                                last.then_inc(flipped, 1)

                            def sums(of, lhs, to):
                                if of.at(-1).edge:
                                    pe.wait_ge(sumT_ready, count_before(of, e0))
                                eq = (same[:, bass.ds(of.pair, 1), :].rearrange("p a c -> p (a c)") if second
                                      else equal[:, w, :])
                                nc.tensor.matmul(to[:, 0:2, :].rearrange("p a c -> p (a c)"), lhs[0],
                                                 eq[:, 0:PAIR], start=True, stop=False)
                                nc.tensor.matmul(to[:, 1, :], lhs[1], eq[:, PAIR:], start=False, stop=True)\
                                    .then_inc(summed, 1)

                            def project(of, weight, to):
                                pe.wait_ge(sumT_ready, count_before(of.at(1), e0))
                                if of.at(-1).edge:
                                    pe.wait_ge(edge_out_ready, count_before(of, e0))
                                for h in range(2):
                                    last = nc.tensor.matmul(to[:, h, :], sumT[:, h, :], weight, start=True, stop=True)
                                last.then_inc(projected, 1)

                            done = now.at(-1)
                            if now.dense or now.edge:
                                pe.wait_ge(h_ready, count_before(now.at(1), 0))
                            if not second:
                                if now.dense:
                                    flip_dense()
                                if done.edge:
                                    project(done, w0_edge[:, :], bank[3])
                                if now.edge:
                                    pe.wait_ge(same_ready, count_before(now.at(1), e0))
                                    sums(now, [H[:, w, 4, :], H[:, w, 5, :]], bank[2])
                                if now.dense:
                                    if now.at(-2).dense:
                                        pe.wait_ge(node_out_ready, count_before(now.at(-1), d0))
                                    y = bank[4 + w]
                                    nc.tensor.matmul(y[:, :, :].rearrange("p a c -> p (a c)"), ones_row[:, :],
                                                     b0_row.rearrange("p a c -> p (a c)"),
                                                     start=True, stop=False)
                                    pe.wait_ge(hT_ready, count_before(now.at(1), d0))
                                    for r in range(ROWS):
                                        last = nc.tensor.matmul(y[:, r, :], hT[:, r, :], w0_node[:, :],
                                                                start=False, stop=(r == ROWS - 1))
                                    last.then_inc(node_made, 1)
                                return
                            if now.edge:
                                pe.wait_ge(side_in[now.slot], uses_of_slot(now, e0) * 16
                                           + (16 if now.last_pair else 0))
                                if now.at(-1).edge:
                                    pe.wait_ge(eT_ready, count_before(now, e0))
                                for c in range(4):
                                    nc.tensor.transpose(bank[0][:, c, :], H[:, w, 4 + c, :], ident[:, :])
                                for h in range(2):
                                    last = nc.tensor.transpose(bank[1][:, h, :], attr[:, now.slot, h, :], ident[:, :])
                                last.then_inc(edge_flipped, 1)
                            if now.dense:
                                flip_dense()
                            if done.edge:
                                pe.wait_ge(msg_ready, count_before(now, e0))
                                sums(done, [msg[:, 0, :], msg[:, 1, :]], bank[3])
                            if now.edge:
                                if now.at(-1).edge:
                                    pe.wait_ge(msg_ready, count_before(now, e0))
                                nc.tensor.matmul(bank[2][:, 0:2, :].rearrange("p a c -> p (a c)"), ones_row[:, :],
                                                 c1_row[:, :, :].rearrange("p a c -> p (a c)"),
                                                 start=True, stop=False)
                                pe.wait_ge(eT_ready, count_before(now.at(1), e0))
                                for h in range(2):
                                    for c, block_of_w in ((2, 0), (0, 1), (4, 2)):
                                        last = nc.tensor.matmul(bank[2][:, h, :], eT[:, c + h, :],
                                                                w1T[:, block_of_w, :], start=False,
                                                                stop=(c == 4 and h == 1))
                                last.then_inc(msg_made, 1)
                            if now.dense:
                                if now.at(-1).dense:
                                    pe.wait_ge(z_link, count_before(now, d0))
                                pe.wait_ge(hT_ready, count_before(now.at(1), d0))
                                for r in range(ROWS):
                                    last = nc.tensor.matmul(bank[6][:, r, :], hT[:, r, :], w2T[:, 0, :],
                                                            start=True, stop=True)
                                last.then_inc(node_made, 1)
                            if done.edge:
                                project(done, w2T[:, 1, :], bank[4])

                        run_steps(pe, plan, tick)

                    both_plans(pe, program)

        def slot2_uses(step, start):
            return uses_in_two(step, start)

        first_lag, second_lag = 3, 6
        layer_phase("nodes1", False, Plan(n_batch, dense0=0, edge0=first_lag), Plan(n_batch, dense0=0))
        layer_phase("edges1", False, None, Plan(n_batch, edge0=0))
        layer_phase("edges2", True, Plan(n_batch, dense0=second_lag, edge0=0), Plan(n_batch, edge0=0))
        layer_phase("nodes2", True, None, Plan(n_batch, dense0=0))


def uses_in_two(step, start):
    per_turn = UNROLL // 2
    first = start + (step.known - start) % 2
    if isinstance(step.turn, int):
        return (step.number - first) // 2 + 1
    return step.turn * per_turn + (step.slot - first) // 2 + 1


_INS = ['x', 'src', 'dst', 'edge_attr_128', 'L0_gnn_W', 'L0_gnn_b', 'L0_gnn_eps', 'L1_gnn_u',
        'L1_gnn_W1', 'L1_gnn_b1', 'L1_gnn_W2', 'L1_gnn_b2']


def kernel(**inputs):
    import numpy as _np
    import concourse.bacc as _bacc
    from concourse import mybir as _mybir
    from concourse.bass_utils import run_bass_kernel_spmd as _run

    nc = _bacc.Bacc("TRN2", target_bir_lowering=False, num_devices=1)
    arrays, args = {}, []
    for name in _INS:
        a = _np.ascontiguousarray(inputs[name])
        arrays[f"in_{name}_dram"] = a
        args.append(nc.dram_tensor(f"in_{name}_dram", a.shape, _mybir.dt.from_np(a.dtype), kind="ExternalInput").ap())
    x = inputs['x']
    out = nc.dram_tensor("out_0_dram", x.shape, _mybir.dt.from_np(_np.dtype('float32')), kind="ExternalOutput").ap()
    gnn_kernel(nc, *args, out)
    r = _run(nc, [arrays], core_ids=[0])
    return r.results[0]["out_0_dram"]
```

```python
from contextlib import ExitStack

import concourse.bass as bass
from concourse import mybir

ALU = mybir.AluOpType
ACT = mybir.ActivationFunctionType
AX = mybir.AxisListType
F32 = mybir.dt.float32
I32 = mybir.dt.int32

P = 128
ROWS = 4
BATCH = P * ROWS
PAIR = 2 * P
UNROLL = 4
BAND_BELOW = 2
BAND_ABOVE = 2
LN_EPS = 1e-5
WARM_UP = 20


class Plan:

    def __init__(self, count, dense0=None, edge0=None):
        self.count, self.dense0, self.edge0 = count, dense0, edge0
        ends = [b + count for b in (dense0, edge0) if b is not None]
        self.steps = max(ends)

    def has_dense(self, s):
        return self.dense0 is not None and self.dense0 <= s < self.dense0 + self.count

    def has_edge(self, s):
        return self.edge0 is not None and self.edge0 <= s < self.edge0 + self.count

    def pattern(self, tick, reach):
        near = []
        for s in range(tick - reach, tick + reach + 1):
            near.append((self.has_dense(s), self.has_edge(s),
                         self.dense0 is not None and s == self.dense0 + self.count - 1,
                         self.edge0 is not None and s == self.edge0 + self.count - 1))
        return near


class Step:

    def __init__(self, plan, turn, slot, known):
        self.plan, self.turn, self.slot, self.known = plan, turn, slot, known

    def at(self, offset):
        s = self.slot + offset
        return Step(self.plan, self.turn + s // UNROLL, s % UNROLL, self.known + offset)

    @property
    def number(self):
        return self.turn * UNROLL + self.slot

    @property
    def dense(self):
        return self.plan.has_dense(self.known)

    @property
    def edge(self):
        return self.plan.has_edge(self.known)

    @property
    def batch(self):
        return self.number - self.plan.dense0

    @property
    def pair(self):
        return self.number - self.plan.edge0

    @property
    def last_batch(self):
        return self.known == self.plan.dense0 + self.plan.count - 1

    @property
    def last_pair(self):
        return self.known == self.plan.edge0 + self.plan.count - 1


def count_before(step, start, per=1):
    return (step.number - start) * per


def uses_of_slot(step, start):
    first = start + (step.known - start) % UNROLL
    return (step.number - first) // UNROLL + 1 if isinstance(step.turn, int) else \
        step.turn + (step.slot - first) // UNROLL + 1


def run_steps(eng, plan, body, reach=7):
    tick, end = -reach, plan.steps + reach
    while tick < end:
        run = tick
        while run < end and plan.pattern(run, reach) == plan.pattern(tick, reach):
            run += 1
        start = tick + (-tick) % UNROLL
        turns = max(0, (run - start) // UNROLL)
        if turns >= 2 and tick >= 0:
            for s in range(tick, start):
                body(Step(plan, s // UNROLL, s % UNROLL, s))
            with eng.Fori(start // UNROLL, start // UNROLL + turns) as turn:
                for slot in range(UNROLL):
                    body(Step(plan, turn, slot, start + slot))
            tick = start + UNROLL * turns
        else:
            body(Step(plan, tick // UNROLL, tick % UNROLL, tick))
            tick += 1


def gnn_kernel(nc, x, src, dst, edge_attr, W0, b0, eps, u, W1, b1, W2, b2, out):
    N, D = x.shape
    E = src.shape[0]
    assert D == P
    n_batch = -(-N // BATCH)
    n_pair = -(-E // PAIR)
    assert n_batch == n_pair <= P
    tail_nodes = N - (n_batch - 1) * BATCH
    tail_rows = next(r for r in range(ROWS, 0, -1) if tail_nodes % (16 * r) == 0)
    tail_parts = tail_nodes // tail_rows
    assert tail_parts <= P
    tail_edges = E - (n_pair - 1) * PAIR
    assert P < tail_edges < PAIR
    pad_edges = n_pair * PAIR - E

    DUMPS = 4
    assert n_pair % 2 == 0
    x1_dram = nc.dram_tensor("x1_scratch", (N + DUMPS * P, D), F32, kind="Internal").ap()
    agg_dram = nc.dram_tensor("agg_scratch", (N + DUMPS * P, D), F32, kind="Internal").ap()
    last_dst = nc.dram_tensor("last_dst", (PAIR,), I32, kind="Internal").ap()

    with ExitStack() as ctx:
        def sb(name, shape, dt=F32):
            return ctx.enter_context(nc.sbuf_tensor(name, shape, dt))

        def sem(name):
            return ctx.enter_context(nc.semaphore(name))

        ident = sb("ident", [P, P])
        later = sb("later", [P, PAIR])
        ones_row = sb("ones_row", [1, P])
        w0_node = sb("w0_node", [P, P])
        w0_edge = sb("w0_edge", [P, P])
        w1T = sb("w1T", [P, 4, P])
        w2T = sb("w2T", [P, 3, P])
        c1_row = sb("c1_row", [1, 2, P])
        c2_fill = sb("c2_fill", [P, ROWS, P])
        eps_ln = sb("eps_ln", [P, 1])
        dst_f = sb("dst_f", [P, n_pair, 2])
        to_dump = sb("to_dump", [P, n_pair, 2])
        index = sb("index", [P, n_pair, 6], I32)
        same = sb("same", [P, n_pair, 3 * P])
        fast = sb("fast", [1, 1], I32)
        landed = sb("landed", [1, n_pair], I32)

        X = sb("X", [P, UNROLL, 8, P])
        H = sb("H", [P, 2, 8, P])
        stats = sb("stats", [P, 2, 8, 6])
        total = sb("total", [P, 2, 8])
        gap = sb("gap", [P, 2, 8])
        spread = sb("spread", [P, 2, 8])
        sd = sb("sd", [P, 2, 8])
        rstd = sb("rstd", [P, 2, 8])
        nmr = sb("nmr", [P, 2, 8])
        hT = sb("hT", [P, ROWS, P])
        eT = sb("eT", [P, 6, P])
        sumT = sb("sumT", [P, 2, P])
        msg = sb("msg", [P, 2, P])
        edge_out = sb("edge_out", [P, 2, 2, P])
        node_out = sb("node_out", [P, 2, ROWS, P])
        agg_in = sb("agg_in", [P, 2, ROWS, P])
        attr = sb("attr", [P, UNROLL, 2, P])
        dst_row = attr[:, :, :, :].rearrange("p s h d -> p s (h d)").bitcast(I32)
        b0_row = agg_in[0:1, 0, :, :]
        masked = agg_in[:, 1, 0:3, :].rearrange("p a c -> p (a c)")
        n_later = sb("n_later", [P, 2, 2])
        moved = sb("moved", [P, 2])
        gather_at = sb("gather_at", [P, UNROLL, 4], I32)
        scatter_at = sb("scatter_at", [P, UNROLL, 2], I32)

        bank = [ctx.enter_context(nc.psum_tensor(f"bank{i}", [P, 4, P], F32)) for i in range(8)]

        w1_in, w2_in = hT, eT
        pair_i = [X[0:n_pair, 0, 0:2, :].bitcast(I32), X[0:n_pair, 0, 2:4, :].bitcast(I32)]
        pair_f = [X[0:n_pair, 1, 0:2, :], X[0:n_pair, 1, 2:4, :]]
        equal = eT[:, :, :].rearrange("p (q c) d -> p q (c d)", q=2)
        u_col = sb("u_col", [P, 1])
        u_wide = H[:, 0, 0, :]
        eps_col = sb("eps_col", [P, 1])
        brow = H[0:1, 1, 0:2, :]
        dump_i = sb("dump_i", [P, DUMPS], I32)
        dump_f = sb("dump_f", [P, DUMPS])
        base_i = sb("base_i", [P, 1], I32)
        base_f = sb("base_f", [P, 1])
        least_f = H[0:1, 1, 2, 0:n_pair]
        overlap = H[0:1, 1, 3, 0:n_pair]
        extreme = H[0:1, 1, 4:6, 0:n_pair]
        least_i = H[0:1, 1, 6, 0:n_pair].bitcast(I32)
        bound = sb("bound", [P, 4])
        ok = sb("ok", [P, 1])
        ones_col = sb("ones_col", [P, 1])
        zeros = H[:, 0, 1:1 + DUMPS, :]
        last_quarter = (n_pair - 1) // 32 * 32

        rows_in = sem("rows_in")
        w_ready = sem("w_ready")
        biased = sem("biased")
        c2_ready = sem("c2_ready")

        with ExitStack() as setup:
            def ssem(name):
                return ctx.enter_context(nc.semaphore(name))

            weights_in = ssem("weights_in")
            b0_in = ssem("b0_in")
            pads_ready = ssem("pads_ready")
            pairs_in = ssem("pairs_in")
            last_kept = ssem("last_kept")
            dump_zeroed = ssem("dump_zeroed")
            pool_consts = ssem("pool_consts")
            dve_consts = ssem("dve_consts")
            pairs_f = ssem("pairs_f")
            bounded = ssem("bounded")
            band_link = ssem("band_link")
            marked = ssem("marked")
            index_turned = ssem("index_turned")
            bounds_turned = ssem("bounds_turned")
            w_turned = ssem("w_turned")
            u_ready = ssem("u_ready")
            one_eps = ssem("one_eps")
            counted = ssem("counted")
            dst_ready = ssem("dst_ready")
            table_link = ssem("table_link")
            block = setup.enter_context(nc.Block())

            @block.sync
            def _(sp):
                sp.wait_ge(pads_ready, 2)
                for t, of in enumerate((src, dst)):
                    sp.dma_start(pair_i[t][0:n_pair - 1],
                                 of[0:(n_pair - 1) * PAIR].rearrange("(q h e) -> q h e", h=2, e=P))\
                      .then_inc(pairs_in, 16)
                    sp.dma_start(pair_i[t][n_pair - 1:n_pair].rearrange("q h e -> q (h e)")[:, 0:tail_edges],
                                 of[(n_pair - 1) * PAIR:E].rearrange("(a e) -> a e", a=1)).then_inc(pairs_in, 16)
                sp.dma_start(w2_in[:, 0:3, :], W2.rearrange("o (c k) -> o c k", c=3)).then_inc(weights_in, 16)
                sp.dma_start(w1_in[:, :, :], W1.rearrange("o (c k) -> o c k", c=4)).then_inc(weights_in, 16)
                sp.dma_start(w0_edge[:, :], W0).then_inc(weights_in, 16)
                with nc.allow_non_contiguous_dma(reason="one vector, a number to a partition"):
                    sp.dma_start(u_col[:, :], u[0:1, :].rearrange("a d -> d a")).then_inc(weights_in, 16)
                sp.dma_start(eps_col[:, :], eps.rearrange("(a d) -> a d", a=1).partition_broadcast(P))\
                  .then_inc(weights_in, 16)
                sp.dma_start(brow[:, 0, :], b1.rearrange("(a d) -> a d", a=1)).then_inc(rows_in, 16)
                sp.dma_start(brow[:, 1, :], b2.rearrange("(a d) -> a d", a=1)).then_inc(rows_in, 16)
                sp.wait_ge(dve_consts, 6)
                for table in (x1_dram, agg_dram):
                    sp.dma_start(table[N:N + DUMPS * P, :].rearrange("(p h) d -> p h d", h=DUMPS), zeros)\
                      .then_inc(dump_zeroed, 16)
                for r in range(ROWS):
                    sp.dma_start(b0_row[:, r, :], b0.rearrange("(a d) -> a d", a=1)).then_inc(b0_in, 16)
                sp.wait_ge(pairs_in, 64)
                sp.dma_start(last_dst.rearrange("(a e) -> a e", a=1),
                             pair_i[1][n_pair - 1:n_pair].rearrange("q h e -> q (h e)")).then_inc(last_kept, 16)
                sp.wait_ge(dump_zeroed, 32)
                sp.wait_ge(b0_in, 16 * ROWS)
                sp.wait_ge(last_kept, 16)

            @block.gpsimd
            def _(pool):
                nc.gpsimd.memset(pair_i[0][last_quarter:n_pair, 1, tail_edges - P:], 0).then_inc(pads_ready, 1)
                nc.gpsimd.iota(pair_i[1][last_quarter:n_pair, 1, tail_edges - P:], pattern=[[1, pad_edges]],
                               base=N + DUMPS * P - pad_edges, channel_multiplier=0).then_inc(pads_ready, 1)
                pool.wait_ge(pads_ready, 2)
                pool.wait_ge(dve_consts, 2)
                nc.gpsimd.affine_select(out=ident[:, :], in_=ident[:, :], compare_op=ALU.not_equal, fill=1.0,
                                        base=0, pattern=[[-1, P]], channel_multiplier=1).then_inc(pool_consts, 1)
                nc.gpsimd.affine_select(out=later[:, :], in_=later[:, :], compare_op=ALU.is_gt, fill=0.0,
                                        base=0, pattern=[[1, PAIR]], channel_multiplier=-1).then_inc(pool_consts, 1)
                nc.gpsimd.iota(dump_i[:, :], pattern=[[P, DUMPS]], base=N,
                               channel_multiplier=1).then_inc(pool_consts, 1)
                nc.gpsimd.iota(base_i[:, :], pattern=[[0, 1]], base=0,
                               channel_multiplier=BATCH).then_inc(pool_consts, 1)
                nc.gpsimd.iota(least_i[:, 0::2], pattern=[[32, n_pair // 2]], base=-32,
                               channel_multiplier=0).then_inc(pool_consts, 1)
                nc.gpsimd.iota(least_i[:, 1::2], pattern=[[32, n_pair // 2]], base=0,
                               channel_multiplier=0).then_inc(pool_consts, 1)

            @block.tensor
            def _(pe):
                pe.wait_ge(pool_consts, 1)
                pe.wait_ge(pairs_f, 2)
                for t in range(2):
                    for h in range(2):
                        last = nc.tensor.transpose(bank[2][:, 2 * t + h, 0:n_pair], pair_f[t][:, h, :],
                                                   ident[0:n_pair, 0:n_pair])
                last.then_inc(index_turned, 1)
                pe.wait_ge(bounded, 2)
                for m in range(2):
                    last = nc.tensor.transpose(bank[4][0:1, 1 + m, 0:n_pair], bound[0:n_pair, m:m + 1],
                                               ident[0:n_pair, 0:n_pair])
                last.then_inc(bounds_turned, 1)
                pe.wait_ge(marked, 1)
                nc.tensor.matmul(bank[5][0:1, 0, 0:1], ok[0:n_pair, :], ones_col[0:n_pair, :],
                                 start=True, stop=True).then_inc(counted, 1)
                pe.wait_ge(weights_in, 80)
                for c in range(3):
                    nc.tensor.transpose(bank[1][:, c, :], w2_in[:, c, :], ident[:, :])
                for c in range(4):
                    last = nc.tensor.transpose(bank[0][:, c, :], w1_in[:, c, :], ident[:, :])
                last.then_inc(w_turned, 1)

            @block.scalar
            def _(act):
                act.wait_ge(dve_consts, 5)
                nc.scalar.activation(sd[:, 0, 0:1], eps_ln[:, :], ACT.Sqrt)

            @block.vector
            def _(dve):
                nc.vector.memset(ident[:, :], 0.0).then_inc(dve_consts, 1)
                nc.vector.memset(later[:, :], 1.0).then_inc(dve_consts, 1)
                nc.vector.memset(ones_col[:, :], 1.0).then_inc(dve_consts, 1)
                nc.vector.memset(ones_row[:, :], 1.0).then_inc(dve_consts, 1)
                nc.vector.memset(eps_ln[:, :], LN_EPS).then_inc(dve_consts, 1)
                nc.vector.memset(zeros, 0.0).then_inc(dve_consts, 1)
                dve.wait_ge(pairs_in, 64)
                for t in range(2):
                    nc.vector.tensor_copy(pair_f[t], pair_i[t]).then_inc(pairs_f, 1)
                dve.wait_ge(pairs_f, 2)
                nc.vector.tensor_reduce(bound[0:n_pair, 0:1], pair_f[1], AX.XY, ALU.max).then_inc(bounded, 1)
                nc.vector.tensor_reduce(bound[0:n_pair, 1:2], pair_f[1], AX.XY, ALU.min).then_inc(bounded, 1)
                dve.wait_ge(index_turned, 1)
                for t in range(2):
                    for h in range(2):
                        nc.vector.tensor_copy(index[:, :, 2 * t + h], bank[2][:, 2 * t + h, 0:n_pair])
                for h in range(2):
                    last = nc.vector.tensor_copy(dst_f[:, :, h], bank[2][:, 2 + h, 0:n_pair])
                last.then_inc(dst_ready, 1)
                dve.wait_ge(pool_consts, 6)
                nc.vector.tensor_copy(base_f[:, :], base_i[:, :]).then_inc(band_link, 1)
                nc.vector.tensor_copy(dump_f[:, :], dump_i[:, :]).then_inc(table_link, 1)
                nc.vector.tensor_copy(least_f, least_i).then_inc(table_link, 1)
                dve.wait_ge(bounded, 2)
                dve.wait_ge(band_link, 1)
                nc.vector.tensor_scalar(bound[0:n_pair, 2:3], bound[0:n_pair, 0:1], base_f[0:n_pair, :],
                                        float((BAND_ABOVE + 1) * BATCH), ALU.subtract, ALU.is_lt).then_inc(band_link, 1)
                nc.vector.tensor_scalar(bound[0:n_pair, 3:4], bound[0:n_pair, 1:2], base_f[0:n_pair, :],
                                        float(-BAND_BELOW * BATCH), ALU.subtract, ALU.is_ge).then_inc(band_link, 1)
                dve.wait_ge(bounds_turned, 1)
                nc.vector.tensor_copy(extreme, bank[4][0:1, 1:3, 0:n_pair]).then_inc(table_link, 1)
                dve.wait_ge(band_link, 3)
                nc.vector.tensor_tensor(ok[0:n_pair, :], bound[0:n_pair, 2:3], bound[0:n_pair, 3:4],
                                        ALU.mult).then_inc(marked, 1)
                dve.wait_ge(dst_ready, 1)
                dve.wait_ge(table_link, 3)
                for d in range(DUMPS):
                    of = (slice(None), slice(d // 2, None, 2), d % 2)
                    nc.vector.tensor_scalar(to_dump[of], dst_f[of], -1.0, dump_f[:, d:d + 1], ALU.mult, ALU.add)
                nc.vector.tensor_tensor(overlap[:, 1:], extreme[:, 1, 1:], extreme[:, 0, 0:n_pair - 1],
                                        ALU.is_le).then_inc(table_link, 1)
                dve.wait_ge(table_link, 4)
                nc.vector.scalar_tensor_tensor(out=landed[:, 1:], in0=overlap[:, 1:], scalar=32.0, in1=least_f[:, 1:],
                                               op0=ALU.mult, op1=ALU.add)
                dve.wait_ge(counted, 1)
                nc.vector.tensor_scalar(fast[:, :], bank[5][0:1, 0, 0:1], float(n_pair) - 0.5, None, ALU.is_ge)
                dve.wait_ge(weights_in, 80)
                nc.vector.tensor_scalar(eps_col[:, :], eps_col[:, :], 1.0, None, ALU.add).then_inc(one_eps, 1)
                nc.vector.tensor_scalar(u_wide, zeros[:, 0, :], u_col[:, :], None, ALU.add).then_inc(u_ready, 1)
                dve.wait_ge(one_eps, 1)
                nc.vector.tensor_scalar(w0_node[:, :], w0_edge[:, :], eps_col[:, :], None, ALU.mult)

        def constant_terms(pe):
            pe.wait_ge(w_ready, 1)
            pe.wait_ge(rows_in, 32)
            for c, wu in enumerate((w1T[:, 3, :], w2T[:, 2, :])):
                nc.tensor.matmul(bank[3][:, c, :], u_wide, wu, start=True, stop=False)
                last = nc.tensor.matmul(bank[3][:, c, :], ones_row[:, :], brow[:, c, :], start=False, stop=True)
            last.then_inc(biased, 1)
            for _ in range(WARM_UP):
                nc.tensor.transpose(bank[7][:, 0, :], ident[:, :], ident[:, :])

        def keep_constant_terms(act):
            nc.scalar.copy(w2T[:, :, :], bank[1][:, 0:3, :])
            nc.scalar.copy(w1T[:, :, :], bank[0][:, :, :]).then_inc(w_ready, 1)
            act.wait_ge(biased, 1)
            for r in range(ROWS):
                last = nc.scalar.copy(c2_fill[:, r, :], bank[3][:, 1, :])
            last.then_inc(c2_ready, 1)
            for r in range(2):
                nc.scalar.copy(c1_row[:, r, :], bank[3][0:1, 0, :])

        def node_rows(table, step):
            if step.last_batch:
                rows = table[N - tail_nodes:N, :].rearrange("(p r) d -> p r d", r=tail_rows)
                return rows, tail_parts, tail_rows
            rows = table[bass.ds(step.batch * BATCH, BATCH), :].rearrange("(p r) d -> p r d", r=ROWS)
            return rows, P, ROWS

        def normalised(step, second):
            lo = 0 if step.dense else 4
            hi = (8 if second else 6) if step.edge else 4
            return lo, hi

        semaphores = {}

        def layer_phase(name, second, fast_plan, slow_plan):
            with ExitStack() as scope:
                def psem(what, of=None):
                    key = f"{of or layer}_{what}"
                    if key not in semaphores:
                        semaphores[key] = ctx.enter_context(nc.semaphore(key))
                    return semaphores[key]

                layer = "second" if second else "first"

                x_in = [psem(f"x_in{i}") for i in range(UNROLL)]
                edge_in = [psem(f"edge_in{i}") for i in range(UNROLL)]
                side_in = [psem(f"side_in{i}") for i in range(UNROLL)]
                agg_loaded = [psem(f"agg_loaded{i}") for i in range(2)]
                stored = [psem(f"stored{i}") for i in range(2)]
                filled = psem("filled")
                scattered = [psem(f"scattered{i}") for i in range(2)]
                staged = psem("staged")
                placed = psem("placed")
                same_ready = psem("same_ready")
                same_kept = psem("same_kept")
                stat_link = psem("stat_link", name)
                spread_ready = psem("spread_ready", name)
                sd_ready = psem("sd_ready", name)
                rstd_link = psem("rstd_link", name)
                coef_ready = psem("coef_ready", name)
                h_ready = psem("h_ready", name)
                flipped = psem("flipped")
                hT_ready = psem("hT_ready")
                edge_flipped = psem("edge_flipped")
                eT_ready = psem("eT_ready")
                msg_made = psem("msg_made")
                msg_ready = psem("msg_ready")
                summed = psem("summed")
                sumT_ready = psem("sumT_ready")
                projected = psem("projected")
                edge_out_ready = psem("edge_out_ready")
                node_made = psem("node_made")
                z_link = psem("z_link")
                node_out_ready = psem("node_out_ready")
                idx_link = psem("idx_link")
                pool_passed = psem("pool_passed")

                n_src = 4 if second else 2
                gather_lead = 3 if second else 4
                gather_from = x1_dram if second else x
                scatter_to = agg_dram if second else x1_dram

                def wait_scattered(eng, step, e0):
                    eng.wait_ge(scattered[(step.known - e0) % 2], uses_in_two(step, e0) * 32)

                def wait_all_scattered(eng):
                    for parity in range(2):
                        eng.wait_ge(scattered[parity], 32 * (n_pair // 2))

                def both_plans(eng, program):
                    flag = eng.value_load(fast[0:1, 0:1])
                    if slow_plan is None or fast_plan is None:
                        with eng.If(flag != 0 if slow_plan is None else flag == 0):
                            program(slow_plan or fast_plan)
                    else:
                        with eng.If(flag != 0):
                            program(fast_plan)
                        with eng.Else():
                            program(slow_plan)

                block = scope.enter_context(nc.Block())

                @block.sync
                def _(sp):
                    def program(plan):
                        d0, e0 = plan.dense0, plan.edge0

                        def tick(now):
                            if now.dense and second:
                                if now.at(-2).dense:
                                    sp.wait_ge(z_link, count_before(now.at(-1), d0))
                                if e0 is not None:
                                    last_pair = now.at(BAND_ABOVE - d0 + e0)
                                    if last_pair.edge:
                                        if last_pair.at(-1).edge:
                                            wait_scattered(sp, last_pair.at(-1), e0)
                                        wait_scattered(sp, last_pair, e0)
                                    else:
                                        wait_all_scattered(sp)
                                rows, parts, r = node_rows(agg_dram, now)
                                sp.dma_start(agg_in[0:parts, now.slot % 2, 0:r, :], rows)\
                                  .then_inc(agg_loaded[now.slot % 2], 16)
                            ahead = now.at(3)
                            if ahead.dense:
                                if now.at(-1).dense:
                                    sp.wait_ge(node_out_ready, count_before(now, d0))
                                rows, parts, r = node_rows(x1_dram if second else x, ahead)
                                sp.dma_start(X[0:parts, ahead.slot, 0:r, :], rows).then_inc(x_in[ahead.slot], 16)
                            ahead = now.at(2)
                            if ahead.edge and second:
                                if now.at(-2).edge:
                                    sp.wait_ge(edge_flipped, count_before(now.at(-1), e0))
                                if ahead.last_pair:
                                    first = (n_pair - 1) * PAIR
                                    sp.dma_start(attr[:, ahead.slot, 0, :], edge_attr[first:first + P, :])\
                                      .then_inc(side_in[ahead.slot], 16)
                                    sp.dma_start(attr[0:tail_edges - P, ahead.slot, 1, :],
                                                 edge_attr[first + P:E, :]).then_inc(side_in[ahead.slot], 16)
                                else:
                                    rows = edge_attr[bass.ds(ahead.pair * PAIR, PAIR), :]
                                    sp.dma_start(attr[:, ahead.slot, :, :], rows.rearrange("(h e) d -> e h d", h=2))\
                                      .then_inc(side_in[ahead.slot], 16)
                            if ahead.edge and not second:
                                if now.at(-2).edge:
                                    sp.wait_ge(same_ready, count_before(now.at(-1), e0))
                                of = last_dst[:] if ahead.last_pair else dst[bass.ds(ahead.pair * PAIR, PAIR)]
                                row = of.rearrange("(a e) -> a e", a=1)
                                sp.dma_start(dst_row[:, ahead.slot, :], row.partition_broadcast(P))\
                                  .then_inc(side_in[ahead.slot], 16)
                            if now.dense and not second:
                                if now.known == d0:
                                    sp.wait_ge(c2_ready, 1)
                                rows, parts, r = node_rows(agg_dram, now)
                                sp.dma_start(rows, c2_fill[0:parts, 0:r, :]).then_inc(filled, 16)
                            done = now.at(-1)
                            if done.dense:
                                sp.wait_ge(node_out_ready, count_before(now, d0))
                                rows, parts, r = node_rows(out if second else x1_dram, done)
                                sp.dma_start(rows, node_out[0:parts, done.slot % 2, 0:r, :])\
                                  .then_inc(stored[done.slot % 2], 16)

                        run_steps(sp, plan, tick)
                        if d0 is not None:
                            for s in range(2):
                                sp.wait_ge(stored[s], 16 * len(range(s, n_batch, 2)))
                            if not second:
                                sp.wait_ge(filled, 16 * n_batch)

                    both_plans(sp, program)

                @block.gpsimd
                def _(pool):
                    def program(plan):
                        d0, e0 = plan.dense0, plan.edge0
                        if e0 is None:
                            return

                        def tick(now):
                            done = now.at(-3 if second else -2)
                            if done.edge:
                                pool.wait_ge(edge_out_ready, count_before(done.at(1), e0))
                                pool.wait_ge(placed, count_before(done.at(1), e0))
                                if done.at(-2).edge:
                                    wait_scattered(pool, done.at(-2), e0)
                                if done.at(-4).edge:
                                    pool.wait_ge(scattered[(done.known - e0 + 1) % 2],
                                                 pool.value_load(landed[0:1, bass.ds(done.pair, 1)],
                                                                 min_val=32, max_val=32 * n_pair))
                                elif done.at(-1).edge:
                                    wait_scattered(pool, done.at(-1), e0)
                                if d0 is not None and not second:
                                    reach = e0 - BAND_ABOVE
                                    whole = done.at(-reach)
                                    if whole.dense:
                                        pool.wait_ge(stored[whole.slot % 2], uses_in_two(whole, d0) * 16)
                                        pool.wait_ge(stored[1 - whole.slot % 2], uses_in_two(whole.at(-1), d0) * 16)
                                    else:
                                        for s in range(2):
                                            pool.wait_ge(stored[s], 16 * len(range(s, n_batch, 2)))
                                pool.sem_inc(pool_passed, 1)
                                for h in range(2):
                                    nc.gpsimd.indirect_dma_start(
                                        out=scatter_to[:, :],
                                        out_offset=bass.IndirectOffsetOnAxis(
                                            ap=scatter_at[:, done.slot, h:h + 1], axis=0),
                                        in_=edge_out[:, done.slot % 2, h, :], in_offset=None,
                                        compute_op=ALU.add).then_inc(scattered[(done.known - e0) % 2], 16)
                            ahead = now.at(gather_lead)
                            if ahead.edge:
                                pool.wait_ge(staged, count_before(ahead.at(1), e0))
                                if ahead.at(-UNROLL).edge:
                                    pool.wait_ge(h_ready, count_before(ahead.at(1 - UNROLL), 0))
                                pool.sem_inc(pool_passed, 1)
                                for c in range(n_src):
                                    nc.gpsimd.indirect_dma_start(
                                        out=X[:, ahead.slot, 4 + c, :], out_offset=None,
                                        in_=gather_from[:, :],
                                        in_offset=bass.IndirectOffsetOnAxis(
                                            ap=gather_at[:, ahead.slot, c:c + 1], axis=0))\
                                        .then_inc(edge_in[ahead.slot], 16)

                        run_steps(pool, plan, tick)
                        wait_all_scattered(pool)

                    both_plans(pool, program)

                @block.vector
                def _(dve):
                    def program(plan):
                        d0, e0 = plan.dense0, plan.edge0

                        def tick(now):
                            done = now.at(-1)
                            w = done.slot % 2
                            if done.dense and second:
                                dve.wait_ge(node_made, count_before(now, d0))
                                if now.at(-3).dense:
                                    dve.wait_ge(stored[w], uses_in_two(now.at(-3), d0) * 16)
                                dve.wait_ge(agg_loaded[w], uses_in_two(done, d0) * 16)
                                nc.vector.tensor_tensor(node_out[:, w, :, :], bank[6][:, :, :], agg_in[:, w, :, :],
                                                        ALU.add).then_inc(z_link, 1)
                                dve.wait_ge(z_link, count_before(now, d0))
                                nc.vector.scalar_tensor_tensor(out=node_out[:, w, :, :], in0=node_out[:, w, :, :],
                                                               scalar=0.0, in1=X[:, done.slot, 0:ROWS, :],
                                                               op0=ALU.max, op1=ALU.add)\
                                    .then_inc(node_out_ready, 1)
                            older = now.at(-2)
                            if older.edge and second:
                                dve.wait_ge(projected, count_before(now.at(-1), e0))
                                if now.at(-4).edge:
                                    wait_scattered(dve, now.at(-3).at(-1), e0)
                                nc.vector.tensor_copy(edge_out[:, older.slot % 2, :, :], bank[4][:, 0:2, :])\
                                    .then_inc(edge_out_ready, 1)
                            if done.edge and second:
                                if now.at(-5).edge:
                                    wait_scattered(dve, now.at(-4).at(-1), e0)
                                nc.vector.tensor_copy(scatter_at[:, done.slot, :],
                                                      index[:, bass.ds(done.pair, 1), 4:6]
                                                      .rearrange("p a c -> p (a c)")).then_inc(placed, 1)
                            ahead = now.at(gather_lead + 1)
                            if ahead.edge:
                                last_use = ahead.at(-UNROLL)
                                if last_use.edge:
                                    dve.wait_ge(edge_in[ahead.slot], uses_of_slot(last_use, e0) * 16 * n_src)
                                nc.vector.tensor_copy(gather_at[:, ahead.slot, 0:n_src],
                                                      index[:, bass.ds(ahead.pair, 1), 0:n_src]
                                                      .rearrange("p a c -> p (a c)")).then_inc(staged, 1)
                            far, near = now.at(2), now.at(1)
                            lo, hi = normalised(far, second)
                            q, v = far.slot % 2, near.slot % 2
                            has_far = far.dense or far.edge
                            compare = near.edge and not second
                            st = stats[:, q, lo:hi, :]
                            line, eq = dst_row[:, near.slot, :], equal[:, v, :]
                            if compare:
                                mine = dst_f[:, bass.ds(near.pair, 1), :].rearrange("p a c -> p (a c)")
                                away = to_dump[:, bass.ds(near.pair, 1), :].rearrange("p a c -> p (a c)")
                                row = index[:, bass.ds(near.pair, 1), 4:6].rearrange("p a c -> p (a c)")
                            if has_far:
                                if far.dense:
                                    dve.wait_ge(x_in[far.slot], uses_of_slot(far, d0) * 16)
                                if far.edge:
                                    dve.wait_ge(edge_in[far.slot], uses_of_slot(far, e0) * 16 * n_src)
                                for t in range(lo, hi):
                                    last = nc.vector.bn_stats(stats[:, q, t, :], X[:, far.slot, t, :])
                                last.then_inc(stat_link, 1)
                            if compare:
                                dve.wait_ge(side_in[near.slot], uses_of_slot(near, e0) * 16)
                                if now.at(-1).edge:
                                    dve.wait_ge(summed, count_before(now, e0))
                                    dve.wait_ge(same_kept, count_before(now, e0))
                                nc.vector.tensor_scalar(eq[:, 0:PAIR], line, mine[:, 0:1], None, ALU.is_equal)
                                nc.vector.tensor_scalar(eq[:, PAIR:], line[:, P:], mine[:, 1:2], None,
                                                        ALU.is_equal).then_inc(same_ready, 1)
                            if has_far:
                                dve.wait_ge(stat_link, count_before(far, 0, 3) + 1)
                                nc.vector.tensor_tensor(gap[:, q, lo:hi], st[:, :, 1], st[:, :, 4], ALU.subtract)\
                                    .then_inc(stat_link, 1)
                                nc.vector.tensor_tensor(total[:, q, lo:hi], st[:, :, 1], st[:, :, 4], ALU.add)
                                nc.vector.tensor_tensor(spread[:, q, lo:hi], st[:, :, 2], st[:, :, 5], ALU.add)
                            if compare:
                                dve.wait_ge(same_ready, count_before(near.at(1), e0))
                                nc.vector.tensor_tensor_reduce(masked[:, 0:PAIR], eq[:, 0:PAIR], later[:, :], 1.0,
                                                               0.0, ALU.mult, ALU.add, n_later[:, v, 0:1])
                            if has_far:
                                dve.wait_ge(stat_link, count_before(far, 0, 3) + 2)
                                nc.vector.scalar_tensor_tensor(out=gap[:, q, lo:hi], in0=gap[:, q, lo:hi],
                                                               scalar=P / 4.0, in1=gap[:, q, lo:hi],
                                                               op0=ALU.mult, op1=ALU.mult).then_inc(stat_link, 1)
                            if compare:
                                nc.vector.tensor_tensor_reduce(masked[:, PAIR:PAIR + P], eq[:, PAIR:], later[:, 0:P],
                                                               1.0, 0.0, ALU.mult, ALU.add, n_later[:, v, 1:2])\
                                    .then_inc(idx_link, 1)
                            if has_far:
                                dve.wait_ge(stat_link, count_before(far.at(1), 0, 3))
                                nc.vector.tensor_tensor(spread[:, q, lo:hi], spread[:, q, lo:hi],
                                                        gap[:, q, lo:hi], ALU.add).then_inc(spread_ready, 1)
                            if now.dense and not second:
                                dve.wait_ge(node_made, count_before(now.at(1), d0))
                                if now.at(-2).dense:
                                    dve.wait_ge(stored[now.slot % 2], uses_in_two(now.at(-2), d0) * 16)
                                nc.vector.tensor_tensor(node_out[:, now.slot % 2, :, :],
                                                        bank[4 + now.slot % 2][:, :, :],
                                                        X[:, now.slot, 0:ROWS, :], ALU.add)\
                                    .then_inc(node_out_ready, 1)
                            if compare:
                                dve.wait_ge(idx_link, count_before(near, e0, 3) + 1)
                                nc.vector.scalar_tensor_tensor(out=moved[:, :], in0=n_later[:, v, :], scalar=1.0,
                                                               in1=away, op0=ALU.min, op1=ALU.mult)\
                                    .then_inc(idx_link, 1)
                            if has_far:
                                dve.wait_ge(sd_ready, count_before(far.at(1), 0))
                                nc.vector.reciprocal(rstd[:, q, lo:hi], sd[:, q, lo:hi]).then_inc(rstd_link, 1)
                            if compare:
                                if now.at(-3).edge:
                                    wait_scattered(dve, now.at(-2).at(-1), e0)
                                dve.wait_ge(idx_link, count_before(near, e0, 3) + 2)
                                nc.vector.tensor_tensor(scatter_at[:, near.slot, :], moved[:, :], mine, ALU.add)\
                                    .then_inc(placed, 1)
                                nc.vector.tensor_tensor(row, moved[:, :], mine, ALU.add).then_inc(idx_link, 1)
                            if has_far:
                                dve.wait_ge(rstd_link, count_before(far.at(1), 0))
                                nc.vector.scalar_tensor_tensor(out=nmr[:, q, lo:hi], in0=total[:, q, lo:hi],
                                                               scalar=-0.5, in1=rstd[:, q, lo:hi],
                                                               op0=ALU.mult, op1=ALU.mult).then_inc(coef_ready, 1)

                        run_steps(dve, plan, tick)

                    both_plans(dve, program)

                @block.scalar
                def _(act):
                    if name == "nodes1":
                        keep_constant_terms(act)

                    def program(plan):
                        d0, e0 = plan.dense0, plan.edge0

                        def tick(now):
                            nxt, later_step = now.at(1), now.at(2)
                            w = now.slot % 2

                            def deviation():
                                lo, hi = normalised(later_step, second)
                                r = later_step.slot % 2
                                act.wait_ge(spread_ready, count_before(now.at(3), 0))
                                nc.scalar.activation(sd[:, r, lo:hi], spread[:, r, lo:hi], ACT.Sqrt,
                                                     bias=eps_ln[:, :], scale=1.0 / P).then_inc(sd_ready, 1)

                            def normalise(part, parts):
                                if not (nxt.dense or nxt.edge):
                                    return
                                lo, hi = normalised(nxt, second)
                                q = nxt.slot % 2
                                if part == 0:
                                    act.wait_ge(coef_ready, count_before(nxt.at(1), 0))
                                    if now.at(-1).dense:
                                        act.wait_ge(flipped, count_before(now, d0))
                                    if now.at(-1).edge:
                                        act.wait_ge(edge_flipped if second else summed, count_before(now, e0))
                                for t in range(lo + (hi - lo) * part // parts, lo + (hi - lo) * (part + 1) // parts):
                                    last = nc.scalar.activation(H[:, q, t, :], X[:, nxt.slot, t, :], ACT.Relu,
                                                                bias=nmr[:, q, t:t + 1], scale=rstd[:, q, t:t + 1])
                                if part == parts - 1:
                                    last.then_inc(h_ready, 1)

                            def copy_hT():
                                act.wait_ge(flipped, count_before(now.at(1), d0))
                                if now.at(-1).dense:
                                    act.wait_ge(node_made, count_before(now, d0))
                                nc.scalar.copy(hT[:, :, :], bank[w if not second else 5][:, :, :])\
                                    .then_inc(hT_ready, 1)

                            def copy_sumT(of):
                                act.wait_ge(summed, count_before(of.at(1), e0))
                                if of.at(-1).edge:
                                    act.wait_ge(projected, count_before(of, e0))
                                nc.scalar.copy(sumT[:, :, :], bank[3 if second else 2][:, 0:2, :])\
                                    .then_inc(sumT_ready, 1)

                            done = now.at(-1)
                            if not second:
                                if now.dense:
                                    copy_hT()
                                normalise(0, 2)
                                if done.edge:
                                    act.wait_ge(projected, count_before(now, e0))
                                    if now.at(-3).edge:
                                        wait_scattered(act, now.at(-2).at(-1), e0)
                                    nc.scalar.copy(edge_out[:, done.slot % 2, :, :], bank[3][:, 0:2, :])\
                                        .then_inc(edge_out_ready, 1)
                                normalise(1, 2)
                                if later_step.dense or later_step.edge:
                                    deviation()
                                if now.edge:
                                    copy_sumT(now)
                                if now.edge:
                                    act.wait_ge(same_ready, count_before(now.at(1), e0))
                                    nc.scalar.copy(same[:, bass.ds(now.pair, 1), :].rearrange("p a c -> p (a c)"),
                                                   equal[:, w, :]).then_inc(same_kept, 1)
                                return
                            if now.dense and not now.edge:
                                copy_hT()
                            normalise(0, 3)
                            if now.edge:
                                act.wait_ge(edge_flipped, count_before(now.at(1), e0))
                                if now.at(-1).edge:
                                    act.wait_ge(msg_made, count_before(now, e0))
                                nc.scalar.copy(eT[:, 0:4, :], bank[0][:, :, :])
                                nc.scalar.copy(eT[:, 4:6, :], bank[1][:, 0:2, :]).then_inc(eT_ready, 1)
                            if now.dense and now.edge:
                                copy_hT()
                            normalise(1, 3)
                            if done.edge:
                                copy_sumT(done)
                            normalise(2, 3)
                            if later_step.dense or later_step.edge:
                                deviation()
                            if now.edge:
                                act.wait_ge(msg_made, count_before(now.at(1), e0))
                                if now.at(-1).edge:
                                    act.wait_ge(summed, count_before(now, e0))
                                nc.scalar.activation(msg[:, :, :], bank[2][:, 0:2, :], ACT.Relu)\
                                    .then_inc(msg_ready, 1)

                        run_steps(act, plan, tick)

                    both_plans(act, program)

                @block.tensor
                def _(pe):
                    if name == "nodes1":
                        constant_terms(pe)

                    def program(plan):
                        d0, e0 = plan.dense0, plan.edge0

                        def tick(now):
                            w = now.slot % 2

                            def flip_dense():
                                if now.at(-1).dense:
                                    pe.wait_ge(hT_ready, count_before(now, d0))
                                for r in range(ROWS):
                                    last = nc.tensor.transpose(bank[5 if second else w][:, r, :],
                                                               H[:, w, r, :], ident[:, :])
                                last.then_inc(flipped, 1)

                            def sums(of, lhs, to):
                                if of.at(-1).edge:
                                    pe.wait_ge(sumT_ready, count_before(of, e0))
                                eq = (same[:, bass.ds(of.pair, 1), :].rearrange("p a c -> p (a c)") if second
                                      else equal[:, w, :])
                                nc.tensor.matmul(to[:, 0:2, :].rearrange("p a c -> p (a c)"), lhs[0],
                                                 eq[:, 0:PAIR], start=True, stop=False)
                                nc.tensor.matmul(to[:, 1, :], lhs[1], eq[:, PAIR:], start=False, stop=True)\
                                    .then_inc(summed, 1)

                            def project(of, weight, to):
                                pe.wait_ge(sumT_ready, count_before(of.at(1), e0))
                                if of.at(-1).edge:
                                    pe.wait_ge(edge_out_ready, count_before(of, e0))
                                for h in range(2):
                                    last = nc.tensor.matmul(to[:, h, :], sumT[:, h, :], weight, start=True, stop=True)
                                last.then_inc(projected, 1)

                            done = now.at(-1)
                            if now.dense or now.edge:
                                pe.wait_ge(h_ready, count_before(now.at(1), 0))
                            if not second:
                                if now.dense:
                                    flip_dense()
                                if done.edge:
                                    project(done, w0_edge[:, :], bank[3])
                                if now.edge:
                                    pe.wait_ge(same_ready, count_before(now.at(1), e0))
                                    sums(now, [H[:, w, 4, :], H[:, w, 5, :]], bank[2])
                                if now.dense:
                                    if now.at(-2).dense:
                                        pe.wait_ge(node_out_ready, count_before(now.at(-1), d0))
                                    y = bank[4 + w]
                                    nc.tensor.matmul(y[:, :, :].rearrange("p a c -> p (a c)"), ones_row[:, :],
                                                     b0_row.rearrange("p a c -> p (a c)"),
                                                     start=True, stop=False)
                                    pe.wait_ge(hT_ready, count_before(now.at(1), d0))
                                    for r in range(ROWS):
                                        last = nc.tensor.matmul(y[:, r, :], hT[:, r, :], w0_node[:, :],
                                                                start=False, stop=(r == ROWS - 1))
                                    last.then_inc(node_made, 1)
                                return
                            if now.edge:
                                pe.wait_ge(side_in[now.slot], uses_of_slot(now, e0) * 16
                                           + (16 if now.last_pair else 0))
                                if now.at(-1).edge:
                                    pe.wait_ge(eT_ready, count_before(now, e0))
                                for c in range(4):
                                    nc.tensor.transpose(bank[0][:, c, :], H[:, w, 4 + c, :], ident[:, :])
                                for h in range(2):
                                    last = nc.tensor.transpose(bank[1][:, h, :], attr[:, now.slot, h, :], ident[:, :])
                                last.then_inc(edge_flipped, 1)
                            if now.dense:
                                flip_dense()
                            if done.edge:
                                pe.wait_ge(msg_ready, count_before(now, e0))
                                sums(done, [msg[:, 0, :], msg[:, 1, :]], bank[3])
                            if now.edge:
                                if now.at(-1).edge:
                                    pe.wait_ge(msg_ready, count_before(now, e0))
                                nc.tensor.matmul(bank[2][:, 0:2, :].rearrange("p a c -> p (a c)"), ones_row[:, :],
                                                 c1_row[:, :, :].rearrange("p a c -> p (a c)"),
                                                 start=True, stop=False)
                                pe.wait_ge(eT_ready, count_before(now.at(1), e0))
                                for h in range(2):
                                    for c, block_of_w in ((2, 0), (0, 1), (4, 2)):
                                        last = nc.tensor.matmul(bank[2][:, h, :], eT[:, c + h, :],
                                                                w1T[:, block_of_w, :], start=False,
                                                                stop=(c == 4 and h == 1))
                                last.then_inc(msg_made, 1)
                            if now.dense:
                                if now.at(-1).dense:
                                    pe.wait_ge(z_link, count_before(now, d0))
                                pe.wait_ge(hT_ready, count_before(now.at(1), d0))
                                for r in range(ROWS):
                                    last = nc.tensor.matmul(bank[6][:, r, :], hT[:, r, :], w2T[:, 0, :],
                                                            start=True, stop=True)
                                last.then_inc(node_made, 1)
                            if done.edge:
                                project(done, w2T[:, 1, :], bank[4])

                        run_steps(pe, plan, tick)

                    both_plans(pe, program)

        first_lag, second_lag = 3, 6
        layer_phase("nodes1", False, Plan(n_batch, dense0=0, edge0=first_lag), Plan(n_batch, dense0=0))
        layer_phase("edges1", False, None, Plan(n_batch, edge0=0))
        layer_phase("edges2", True, Plan(n_batch, dense0=second_lag, edge0=0), Plan(n_batch, edge0=0))
        layer_phase("nodes2", True, None, Plan(n_batch, dense0=0))


def uses_in_two(step, start):
    per_turn = UNROLL // 2
    first = start + (step.known - start) % 2
    if isinstance(step.turn, int):
        return (step.number - first) // 2 + 1
    return step.turn * per_turn + (step.slot - first) // 2 + 1


_INS = ['x', 'src', 'dst', 'edge_attr_128', 'L0_gnn_W', 'L0_gnn_b', 'L0_gnn_eps', 'L1_gnn_u',
        'L1_gnn_W1', 'L1_gnn_b1', 'L1_gnn_W2', 'L1_gnn_b2']


def kernel(**inputs):
    import numpy as _np
    import concourse.bacc as _bacc
    from concourse import mybir as _mybir
    from concourse.bass_utils import run_bass_kernel_spmd as _run

    nc = _bacc.Bacc("TRN2", target_bir_lowering=False, num_devices=1)
    arrays, args = {}, []
    for name in _INS:
        a = _np.ascontiguousarray(inputs[name])
        arrays[f"in_{name}_dram"] = a
        args.append(nc.dram_tensor(f"in_{name}_dram", a.shape, _mybir.dt.from_np(a.dtype), kind="ExternalInput").ap())
    x = inputs['x']
    out = nc.dram_tensor("out_0_dram", x.shape, _mybir.dt.from_np(_np.dtype('float32')), kind="ExternalOutput").ap()
    gnn_kernel(nc, *args, out)
    r = _run(nc, [arrays], core_ids=[0])
    return r.results[0]["out_0_dram"]
```
